# Optimizing a Trainium2 kernel written in Bass

```python
import numpy as np
import jax
import jax.numpy as jnp

def _softmax(x, axis=-1):
    return jax.nn.softmax(x, axis=axis)

def _gelu(x):
    return jax.nn.gelu(x, approximate=True)

def _silu(x):
    return jax.nn.silu(x)

def _sigmoid(x):
    return jax.nn.sigmoid(x)

def _layernorm(x, axis=-1, eps=1e-05):
    m = jnp.mean(x, axis=axis, keepdims=True)
    v = jnp.var(x, axis=axis, keepdims=True)
    return (x - m) / jnp.sqrt(v + eps)

def _scatter_add(tgt, idx, src, axis=0):
    return tgt.at[idx].add(src)

def _segment_sum(src, seg, n):
    return jax.ops.segment_sum(src, seg, n)
kernel_name = 'mk_sandwich_d1_jaxref_r8_c86aa6'

def setup_inputs(seed: int=0):
    np.random.seed(seed)
    _w = jnp.asarray

    def _L0_attn_setup():
        import jax, jax.numpy as jnp
        import numpy as np
        NUM_HEADS = 16
        EPS = 1e-05
        key = jax.random.key(seed)
        k1, k2, k3 = jax.random.split(key, 3)
        b, n, d = (2, 256, 128)
        x = jax.random.normal(k1, (b, n, d), dtype=jnp.float32)
        wqkv = jax.random.normal(k2, (d, 3 * d), dtype=jnp.float32) * (1.0 / np.sqrt(d))
        wo = jax.random.normal(k3, (d, d), dtype=jnp.float32) * (1.0 / np.sqrt(d))
        return {'x': x, 'wqkv': wqkv, 'wo': wo}
    _L0_attn_in = _L0_attn_setup()

    def _L0_ffn_setup():
        import jax, jax.numpy as jnp
        import numpy as np
        L, E, H, F, K = (4, 4, 128, 512, 2)
        B, S = (4, 256)
        EPS = 1e-05

        def _moe_layer(x, rw, rb, g, b, w1, b1, w2, b2):
            logits = jnp.einsum('bsh,he->bse', x, rw) + rb
            probs = jax.nn.softmax(logits, axis=-1)
            vals, idx = jax.lax.top_k(probs, K)
            vals = vals / vals.sum(axis=-1, keepdims=True)
            mu = x.mean(axis=-1, keepdims=True)
            xc = x - mu
            xhat = xc * jax.lax.rsqrt((xc * xc).mean(axis=-1, keepdims=True) + EPS)
            xe = xhat[None] * g[:, None, None, :] + b[:, None, None, :]
            h = jax.nn.gelu(jnp.einsum('ebsh,ehf->ebsf', xe, w1) + b1[:, None, None, :], approximate=False)
            y = jnp.einsum('ebsf,efh->ebsh', h, w2) + b2[:, None, None, :]
            expert_out = x[None] + y
            comb = jnp.einsum('bsk,bske->bse', vals, jax.nn.one_hot(idx, E, dtype=x.dtype))
            return jnp.einsum('bse,ebsh->bsh', comb, expert_out)
        key = jax.random.key(seed)
        ks = jax.random.split(key, 4)
        return {'hidden_states': jax.random.normal(ks[0], (B, S, H), jnp.float32), 'router_w': 0.02 * jax.random.normal(ks[1], (L, H, E), jnp.float32), 'router_b': jnp.zeros((L, E), jnp.float32), 'ln_g': jnp.ones((L, E, H), jnp.float32), 'ln_b': jnp.zeros((L, E, H), jnp.float32), 'w1': 0.02 * jax.random.normal(ks[2], (L, E, H, F), jnp.float32), 'b1': jnp.zeros((L, E, F), jnp.float32), 'w2': 0.02 * jax.random.normal(ks[3], (L, E, F, H), jnp.float32), 'b2': jnp.zeros((L, E, H), jnp.float32)}
    _L0_ffn_in = _L0_ffn_setup()
    _d = {'L0_attn_x': _L0_attn_in['x'], 'L0_attn_wqkv': _L0_attn_in['wqkv'], 'L0_attn_wo': _L0_attn_in['wo'], 'L0_ffn_router_w': _L0_ffn_in['router_w'], 'L0_ffn_router_b': _L0_ffn_in['router_b'], 'L0_ffn_ln_g': _L0_ffn_in['ln_g'], 'L0_ffn_ln_b': _L0_ffn_in['ln_b'], 'L0_ffn_w1': _L0_ffn_in['w1'], 'L0_ffn_b1': _L0_ffn_in['b1'], 'L0_ffn_w2': _L0_ffn_in['w2'], 'L0_ffn_b2': _L0_ffn_in['b2']}
    _x0 = _d['L0_attn_x']
    _d['L0_attn_x'] = jax.random.normal(jax.random.fold_in(jax.random.key(seed), 1), (32, 256, 128), dtype=_x0.dtype)
    del _x0
    return _d

def reference(L0_attn_x, L0_attn_wqkv, L0_attn_wo, L0_ffn_router_w, L0_ffn_router_b, L0_ffn_ln_g, L0_ffn_ln_b, L0_ffn_w1, L0_ffn_b1, L0_ffn_w2, L0_ffn_b2):

    def _L0_attn_ref(x, wqkv, wo):
        import jax, jax.numpy as jnp
        import numpy as np
        NUM_HEADS = 16
        EPS = 1e-05
        b, n, d = x.shape
        h = NUM_HEADS
        hd = d // h
        qkv = x @ wqkv
        q, k, v = jnp.split(qkv, 3, axis=-1)
        q = jax.nn.relu(q)
        k = jax.nn.relu(k)
        split_heads = lambda t: t.reshape(b, n, h, hd).transpose(0, 2, 1, 3)
        q, k, v = (split_heads(q), split_heads(k), split_heads(v))
        kv = jnp.cumsum(k[..., :, None] * v[..., None, :], axis=2)
        num = jnp.einsum('bhnd,bhnde->bhne', q, kv)
        k_sum = jnp.cumsum(k, axis=2)
        den = jnp.einsum('bhnd,bhnd->bhn', q, k_sum)[..., None] + EPS
        y = num / den
        y = y.transpose(0, 2, 1, 3).reshape(b, n, d)
        return y @ wo

    def _L0_ffn_ref(hidden_states, router_w, router_b, ln_g, ln_b, w1, b1, w2, b2):
        import jax, jax.numpy as jnp
        import numpy as np
        L, E, H, F, K = (4, 4, 128, 512, 2)
        B, S = (4, 256)
        EPS = 1e-05

        def _moe_layer(x, rw, rb, g, b, w1, b1, w2, b2):
            logits = jnp.einsum('bsh,he->bse', x, rw) + rb
            probs = jax.nn.softmax(logits, axis=-1)
            vals, idx = jax.lax.top_k(probs, K)
            vals = vals / vals.sum(axis=-1, keepdims=True)
            mu = x.mean(axis=-1, keepdims=True)
            xc = x - mu
            xhat = xc * jax.lax.rsqrt((xc * xc).mean(axis=-1, keepdims=True) + EPS)
            xe = xhat[None] * g[:, None, None, :] + b[:, None, None, :]
            h = jax.nn.gelu(jnp.einsum('ebsh,ehf->ebsf', xe, w1) + b1[:, None, None, :], approximate=False)
            y = jnp.einsum('ebsf,efh->ebsh', h, w2) + b2[:, None, None, :]
            expert_out = x[None] + y
            comb = jnp.einsum('bsk,bske->bse', vals, jax.nn.one_hot(idx, E, dtype=x.dtype))
            return jnp.einsum('bse,ebsh->bsh', comb, expert_out)
        x = hidden_states
        for l in range(L):
            x = _moe_layer(x, router_w[l], router_b[l], ln_g[l], ln_b[l], w1[l], b1[l], w2[l], b2[l])
        return x
    x = L0_attn_x
    x = x + _layernorm(_L0_attn_ref(_layernorm(x, axis=-1), L0_attn_wqkv, L0_attn_wo), axis=-1)
    x = x + _layernorm(_L0_ffn_ref(_layernorm(x, axis=-1), L0_ffn_router_w, L0_ffn_router_b, L0_ffn_ln_g, L0_ffn_ln_b, L0_ffn_w1, L0_ffn_b1, L0_ffn_w2, L0_ffn_b2), axis=-1)
    return x

_drawn_inputs = setup_inputs


def setup_inputs(seed=0):
    import zlib

    import numpy as np

    out = dict(_drawn_inputs(seed))
    spreads = {'L0_ffn_router_b': (0.0, 0.1),
     'L0_ffn_ln_g': (1.0, 0.6),
     'L0_ffn_ln_b': (0.0, 0.8),
     'L0_ffn_b1': (0.0, 0.535),
     'L0_ffn_b2': (0.0, 0.1)}
    factors = {}
    for name, (base, spread) in spreads.items():
        noise = np.random.default_rng([zlib.crc32(name.encode()), seed]).standard_normal(out[name].shape)
        drawn = base * np.exp(spread * noise) if base else spread * noise
        out[name] = jnp.asarray(drawn.astype(out[name].dtype))
    for name, factor in factors.items():
        out[name] = (out[name] * factor).astype(out[name].dtype)
    return out
```

```python
import concourse.bass as bass
from concourse import mybir
from contextlib import ExitStack

F32 = mybir.dt.float32
F32R = mybir.dt.float32r
ALU = mybir.AluOpType
ACT = mybir.ActivationFunctionType
AX = mybir.AxisListType
ds = bass.ds

P = 128
BATCH, SEQ, D = 32, 256, 128
TOKENS = BATCH * SEQ
TILE = 512
NT = TOKENS // TILE
NB = TILE // P
HEADS, HD = 16, 8
G = 4
J = HEADS // G
L, E, F, FC = 4, 4, 512, 4
K = E * FC
EPS = 1e-5
TINY, NEVER = 1.2e-38, 3.0e38
HBUF = 4
LEAD = 3


def sandwich_kernel(nc, x, wqkv, wo, router_w, router_b, ln_g, ln_b, w1, b1, w2, b2, out):
    ctx = ExitStack()
    with ctx:
        def sb(name, shape, dt=F32, to=ctx):
            return to.enter_context(nc.sbuf_tensor(name, shape, dt))

        def sem(name):
            return ctx.enter_context(nc.semaphore(name))

        x1 = sb("x1", [P, NT * TILE])
        u = sb("u", [P, NT * TILE])
        w1s = sb("w1s", [P, L * E * F])
        w2s = sb("w2s", [P, E * FC * D])
        ident = sb("ident", [P, P])
        rows = sb("rows", [112, P])
        cols = sb("cols", [P, 112])
        b1f = sb("b1f", [P, L * K])
        rw = sb("rw", [P, L * E])
        rwp = sb("rwp", [P, L * 2 * E], F32R)
        cs = sb("cs", [P, L * E])
        rb = sb("rb", [P, L * E])
        onesf = sb("onesf", [P, P])
        order = sb("order", [P, E * E])
        half = sb("half", [P, NB])
        epsc = sb("epsc", [P, NB])
        LNG, LNB, B2 = 64, 80, 96

        s_wqkv, s_small, s_w1, s_w2 = sem("wqkv_in"), sem("small_in"), sem("w1_in"), sem("w2_in")
        s_pool0, s_pool1, s_pool2 = sem("pool_memset"), sem("pool_select"), sem("pool_bd")
        s_const = sem("constants_done")
        s_cols_ps, s_cols, s_b1_ps, s_b1f = sem("cols_psum"), sem("cols_ready"), sem("b1_psum"), sem("b1f_ready")
        s_w1g, s_whi, s_wlo = sem("w1_scaled"), sem("w_high"), sem("w_rest")
        s_rwp = sem("router_split")
        s_alone = sem("wait_alone")
        s_x = sem("x_in")
        a_bn, a_mv, a_rs, a_ve, a_xn = sem("a_bn"), sem("a_mv"), sem("a_rstd"), sem("a_ve"), sem("a_xn")
        a_xT_ps, a_xT = sem("a_xT_psum"), sem("a_xT")
        a_q_ps, a_k_ps, a_v_ps, a_kt_ps, a_kv_ps = (sem(f"a_{n}_psum") for n in ("q", "k", "v", "kt", "kv"))
        a_q, a_k, a_v, a_kt, a_kv = (sem(f"a_{n}") for n in ("q", "k", "v", "kt", "kv"))
        a_s_ps, a_s = sem("a_scores_psum"), sem("a_scores")
        a_nd = sem("a_num_den_psum")
        a_den, a_rec, a_y = sem("a_den"), sem("a_rec"), sem("a_y")
        a_o_ps, a_o = sem("a_o_psum"), sem("a_o")
        a_lno = sem("a_ln_o")
        a_x1 = sem("a_x1")
        a_u = sem("a_u")

        x_t = x.rearrange("(t s) n d -> t (s n) d", t=NT)
        x_t = x_t.rearrange("t (b p) d -> t p b d", p=P)
        out_t = out.rearrange("(t s) n d -> t (s n) d", t=NT).rearrange("t (b p) d -> t p b d", p=P)

        def blocks(ap):
            return ap.rearrange("p (b n) -> p b n", b=NB)

        att = ExitStack()
        with att:
            def asb(name, shape, dt=F32):
                return sb(name, shape, dt, att)

            def aps(name):
                return att.enter_context(nc.psum_tensor(name, [P, 512], F32))

            wqkv_sb, wo_sb = asb("wqkv_sb", [P, 3 * D]), asb("wo_sb", [P, D])
            causal = asb("causal", [P, P])
            headbd = asb("headbd", [P, P])
            jmask = asb("jmask", [P, J])
            onesj = asb("onesj", [P, J, 32])
            bn = asb("bn", [P, NB, 6])
            mv = asb("mv", [P, NB, 2])
            ve, rs = asb("ve", [P, NB]), asb("rs", [P, NB])
            xn = asb("xn", [P, TILE])
            xnT = asb("xnT", [P, TILE])
            qT = [asb(f"qT{i}", [P, TILE]) for i in range(2)]
            kT = [asb(f"kT{i}", [P, TILE]) for i in range(2)]
            qx = [asb(f"qx{i}", [P, J, TILE]) for i in range(2)]
            VX = J * (D + HD)
            vx = [asb(f"vx{i}", [P, NB, VX]) for i in range(2)]
            ksum = asb("ksum", [P, 2])
            ktok = asb("ktok", [P, 2, D])
            kvbd = [asb(f"kvbd{i}", [P, 2, D]) for i in range(2)]
            ksbd = [asb(f"ksbd{i}", [P, 2, D]) for i in range(2)]
            sc = [asb(f"sc{i}", [P, G, J * P]) for i in range(2)]
            den, rec, yT = asb("den", [P, TILE]), asb("rec", [P, TILE]), asb("yT", [P, TILE])
            on = asb("on", [P, TILE])
            ps_s = [aps(f"ps_s{g}") for g in range(G)]
            ps_num, ps_den, ps_a, ps_b = aps("ps_num"), aps("ps_den"), aps("ps_a"), aps("ps_b")

            def own_heads(buf, b):
                v = buf[:, b, :].rearrange("p (j n) -> p j n", j=J)[:, :, 0:D]
                return v.rearrange("p j (g x) -> p j g x", g=G)[:, :, :, 0:HD]

            block = att.enter_context(nc.Block())

            @block.sync
            def _(sp):
                sp.dma_start(blocks(x1[:, 0:TILE]), x_t[0]).then_inc(s_x, 16)
                sp.dma_start(wqkv_sb[:], wqkv).then_inc(s_wqkv, 16)
                sp.dma_start(wo_sb[:], wo).then_inc(s_wqkv, 16)
                with sp.Fori(1, NT) as t:
                    sp.wait_ge(s_x, t * 16)
                    sp.dma_start(blocks(x1[:, ds(t * TILE, TILE)]), x_t[ds(t, 1)].rearrange("o p b d -> p (o b) d")).then_inc(s_x, 16)
                sp.dma_start(rows[0:64, :], b1.rearrange("l e (c p) -> (l e c) p", p=P)).then_inc(s_small, 16)
                sp.dma_start(rows[LNG:LNG + 16, :], ln_g.rearrange("l e h -> (l e) h")).then_inc(s_small, 16)
                sp.dma_start(rows[LNB:LNB + 16, :], ln_b.rearrange("l e h -> (l e) h")).then_inc(s_small, 16)
                sp.dma_start(rows[B2:B2 + 16, :], b2.rearrange("l e h -> (l e) h")).then_inc(s_small, 16)
                sp.dma_start(rw[:].rearrange("h (l e) -> h l e", l=L), router_w.rearrange("l h e -> h l e")).then_inc(s_small, 16)
                sp.dma_start(rb[:], router_b.rearrange("l e -> (l e)").partition_broadcast(P)).then_inc(s_small, 16)
                for l in range(L):
                    sp.dma_start(w1s[:, l * E * F:(l + 1) * E * F].rearrange("h (e f) -> h e f", e=E),
                                 w1[l].rearrange("e h f -> h e f")).then_inc(s_w1, 16)
                for e in range(E):
                    sp.dma_start(blocks(w2s[:, e * F:(e + 1) * F]),
                                 w2[0, e].rearrange("(c p) h -> p c h", p=P)).then_inc(s_w2, 16)

            @block.gpsimd
            def _(pool):
                g = nc.gpsimd
                g.memset(ident[:], 0.0)
                g.memset(causal[:], 1.0)
                g.memset(headbd[:], 1.0)
                g.memset(onesj[:], 0.0)
                g.memset(half[:], -0.5)
                g.memset(epsc[:], EPS)
                g.memset(onesf[:], 1.0)
                g.memset(order[:], 0.0).then_inc(s_pool0, 1)
                pool.wait_ge(s_pool0, 1)
                g.affine_select(out=ident[:], in_=ident[:], compare_op=ALU.not_equal, fill=1.0, base=0,
                                pattern=[[-1, P]], channel_multiplier=1)
                g.affine_select(out=causal[:], in_=causal[:], compare_op=ALU.is_ge, fill=0.0, base=0,
                                pattern=[[1, P]], channel_multiplier=-1)
                g.affine_select(out=headbd[:], in_=headbd[:], compare_op=ALU.is_ge, fill=0.0, base=0,
                                pattern=[[-HD, HEADS], [0, HD]], channel_multiplier=1).then_inc(s_pool1, 1)
                for j in range(J):
                    g.memset(onesj[:, j, HD * j:HD * (j + 1)], 1.0)
                for e in range(E):
                    g.memset(order[:, e * E + e:e * E + e + 1], NEVER)
                    if e < E - 1:
                        g.memset(order[:, e * E + e + 1:(e + 1) * E], TINY)
                pool.wait_ge(s_pool1, 1)
                g.affine_select(out=headbd[:], in_=headbd[:], compare_op=ALU.is_ge, fill=0.0, base=HD - 1,
                                pattern=[[HD, HEADS], [0, HD]], channel_multiplier=-1).then_inc(s_const, 1)

                def rstd(n):
                    pool.wait_ge(a_mv, n + 1)
                    g.tensor_tensor(ve[:], mv[:, :, 1], epsc[:], ALU.add).then_inc(a_ve, 1)
                    pool.wait_ge(a_ve, n + 1)
                    g.tensor_tensor(rs[:], ve[:], half[:], ALU.pow).then_inc(a_rs, 1)

                with pool.Fori(0, 3 * NT) as n:
                    rstd(n)

            def layer_norm_stats(dve, src, n):
                for b in range(NB):
                    last = nc.vector.bn_stats(bn[:, b, :], src(b))
                last.then_inc(a_bn, 1)
                dve.wait_ge(a_bn, n + 1).then_inc(s_alone, 1)
                for b in range(NB):
                    last = nc.vector.bn_aggr(mv[:, b, :], bn[:, b, :])
                last.then_inc(a_mv, 1)
                dve.wait_ge(a_rs, n + 1)

            def normed(dst, src, b):
                return nc.vector.tensor_scalar(dst, src, mv[:, b, 0:1], rs[:, b:b + 1], ALU.subtract, ALU.mult)

            @block.vector
            def _(dve):
                v = nc.vector

                def norm_x(t, n):
                    dve.wait_ge(s_x, t * 16 + 16).then_inc(s_alone, 1)
                    layer_norm_stats(dve, lambda b: x1[:, ds(t * TILE + b * P, P)], n)
                    for b in range(NB):
                        last = normed(xn[:, b * P:(b + 1) * P], x1[:, ds(t * TILE + b * P, P)], b)
                    last.then_inc(a_xn, 1)

                def spread_v(t, par):
                    dve.wait_ge(a_v_ps, t + 1)
                    for b in range(NB):
                        last = v.tensor_copy(own_heads(vx[par], b), ps_b[:, b * P:(b + 1) * P].rearrange(
                            "p (g j e) -> p j g e", g=G, j=J))
                    last.then_inc(a_v, 1)

                def state(t, par):
                    dve.wait_ge(a_kv_ps, t + 1)
                    dve.wait_ge(a_k, t + 1)
                    v.tensor_tensor(kvbd[par][:], ps_a[:, 256:512].rearrange("p (s n) -> p s n", s=2),
                                    headbd[:].unsqueeze(1).to_broadcast([P, 2, P]), ALU.mult)
                    for s in range(2):
                        last = v.tensor_scalar(ksbd[par][:, s, :], headbd[:], ksum[:, s:s + 1], None, ALU.mult)
                    last.then_inc(a_kv, 1)

                def mask(t, b, fresh=False):
                    if not fresh:
                        dve.wait_ge(a_nd, t * NB + b - 1)
                    for g in range(G):
                        dve.wait_ge(a_s_ps, t * 16 + b * G + g + 1)
                        v.tensor_tensor(sc[b % 2][:, g, :].rearrange("p (j n) -> p j n", j=J),
                                        ps_s[g][:].rearrange("p (j n) -> p j n", j=J),
                                        causal[:].unsqueeze(1).to_broadcast([P, J, P]), ALU.mult).then_inc(a_s, 1)

                def divide(t):
                    dve.wait_ge(a_nd, t * NB + NB)
                    v.tensor_scalar(den[:], ps_den[:], EPS, None, ALU.add).then_inc(a_den, 1)
                    dve.wait_ge(a_den, t + 1)
                    v.reciprocal(rec[:], den[:]).then_inc(a_rec, 1)
                    dve.wait_ge(a_rec, t + 1)
                    v.tensor_tensor(yT[:], ps_num[:], rec[:], ALU.mult).then_inc(a_y, 1)

                def finish(t, n):
                    dve.wait_ge(a_o_ps, t + 1)
                    layer_norm_stats(dve, lambda b: ps_b[:, b * P:(b + 1) * P], n)
                    for b in range(NB):
                        last = normed(on[:, b * P:(b + 1) * P], ps_b[:, b * P:(b + 1) * P], b)
                    last.then_inc(a_o, 1)
                    dve.wait_ge(a_o, t + 1)
                    xt = x1[:, ds(t * TILE, TILE)]
                    v.tensor_tensor(xt, xt, on[:], ALU.add).then_inc(a_x1, 1)
                    dve.wait_ge(a_x1, t + 1).then_inc(s_alone, 1)
                    layer_norm_stats(dve, lambda b: x1[:, ds(t * TILE + b * P, P)], n + 1)
                    for b in range(NB):
                        last = normed(u[:, ds(t * TILE + b * P, P)], x1[:, ds(t * TILE + b * P, P)], b)
                    last.then_inc(a_u, 1)

                for par in range(2):
                    last = v.memset(vx[par][:], 0.0)
                dve.wait_ge(s_const, 1)
                v.reduce_sum(jmask[:], headbd[:].rearrange("p (g j e) -> p j g e", g=G, j=J)[:, :, :, 0], axis=AX.X).then_inc(s_pool2, 1)
                norm_x(0, 0)
                spread_v(0, 0)
                state(0, 0)

                def body(t, par, prev, nxt, n):
                    mask(t, 0, not prev)
                    if prev:
                        divide(t - 1)
                    if nxt:
                        norm_x(t + 1, n)
                    mask(t, 1, not prev)
                    mask(t, 2)
                    mask(t, 3)
                    if nxt:
                        spread_v(t + 1, 1 - par)
                        state(t + 1, 1 - par)
                    if prev:
                        finish(t - 1, n + (1 if nxt else 0))

                body(0, 0, False, True, 1)
                body(1, 1, True, True, 2)
                with dve.Fori(1, NT // 2 - 1) as q:
                    body(q * 2, 0, True, True, q * 6 - 1)
                    body(q * 2 + 1, 1, True, True, q * 6 + 2)
                body(NT - 2, 0, True, True, 3 * NT - 7)
                body(NT - 1, 1, True, False, 3 * NT - 4)
                divide(NT - 1)
                finish(NT - 1, 3 * NT - 2)

            @block.scalar
            def _(act):
                a = nc.scalar

                def evacuate(t, par):
                    act.wait_ge(a_xT_ps, t + 1)
                    a.activation(xnT[:], ps_a[:], ACT.Identity).then_inc(a_xT, 1)
                    act.wait_ge(a_q_ps, t + 1)
                    a.activation(qT[par][:], ps_b[:], ACT.Relu)
                    for j in range(J):
                        last = a.activation(qx[par][:, j, :], ps_b[:], ACT.Relu, scale=jmask[:, j:j + 1])
                    last.then_inc(a_q, 1)
                    act.wait_ge(a_k_ps, t + 1)
                    for s in range(2):
                        c = s * SEQ
                        a.activation(kT[par][:, c:c + P], ps_a[:, c:c + P], ACT.Relu, accum_out=ksum[:, s:s + 1])
                        last = a.activation(kT[par][:, c + P:c + 2 * P], ps_a[:, c + P:c + 2 * P], ACT.Relu)
                    last.then_inc(a_k, 1)
                    act.wait_ge(a_kt_ps, t + 1)
                    a.activation(ktok[:].rearrange("p s n -> p (s n)"), ps_a[:, 0:256], ACT.Relu).then_inc(a_kt, 1)

                act.wait_ge(s_pool2, 1)
                evacuate(0, 0)

                def body(t, par):
                    act.wait_ge(a_nd, t * NB)
                    evacuate(t + 1, 1 - par)

                evacuate(1, 1)
                with act.Fori(1, NT // 2) as q:
                    body(q * 2 - 1, 1)
                    body(q * 2, 0)

            @block.tensor
            def _(pe):
                mm = nc.tensor.matmul

                def blk(b):
                    return slice(b * P, (b + 1) * P)

                def transposes(t):
                    pe.wait_ge(a_xn, t + 1)
                    for b in range(NB):
                        last = nc.tensor.transpose(ps_a[:, blk(b)], xn[:, blk(b)], ident[:])
                    last.then_inc(a_xT_ps, 1)

                def qk(t):
                    pe.wait_ge(a_xT, t + 1)
                    mm(ps_b[:], wqkv_sb[:, 0:D], xnT[:], start=True, stop=True).then_inc(a_q_ps, 1)
                    mm(ps_a[:], wqkv_sb[:, D:2 * D], xnT[:], start=True, stop=True).then_inc(a_k_ps, 1)

                def vk(t):
                    pe.wait_ge(a_q, t + 1)
                    for b in range(NB):
                        last = mm(ps_b[:, blk(b)], xnT[:, blk(b)], wqkv_sb[:, 2 * D:3 * D], start=True, stop=True)
                    last.then_inc(a_v_ps, 1)
                    pe.wait_ge(a_k, t + 1)
                    for s in range(2):
                        last = mm(ps_a[:, blk(s)], xnT[:, blk(2 * s)], wqkv_sb[:, D:2 * D], start=True, stop=True)
                    last.then_inc(a_kt_ps, 1)

                def kv(t, par):
                    pe.wait_ge(a_kt, t + 1)
                    pe.wait_ge(a_v, t + 1)
                    for s in range(2):
                        moving = own_heads(vx[par], 2 * s).rearrange("p j g e -> p g j e")
                        last = mm(ps_a[:, 256 + s * P:256 + (s + 1) * P].rearrange("p (g j e) -> p g j e", g=G, j=J),
                                  ktok[:, s, :], moving, start=True, stop=True)
                    last.then_inc(a_kv_ps, 1)

                def scores(t, par, b, first):
                    for g in range(G):
                        r = slice(32 * g, 32 * g + 32)
                        if not first:
                            pe.wait_ge(a_s, t * 16 + b * G + g - G + 1)
                        mm(ps_s[g][:].rearrange("p (j n) -> p j n", j=J), kT[par][r, blk(b)], qx[par][r, :, blk(b)],
                           start=True, stop=True).then_inc(a_s_ps, 1)

                def num_den(t, par, b, first):
                    if not first and b == 0:
                        pe.wait_ge(a_y, t)
                    pe.wait_ge(a_s, t * 16 + b * G + G)
                    carried = b % 2
                    if carried:
                        pe.wait_ge(a_kv, t + 1)
                        for ps, st in ((ps_num, kvbd), (ps_den, ksbd)):
                            for g in range(G):
                                r = slice(32 * g, 32 * g + 32)
                                mm(ps[r, blk(b)], st[par][:, b // 2, r], qT[par][:, blk(b)], start=True, stop=False,
                                   skip_group_check=True)
                    for j in range(J):
                        for g in range(G):
                            r = slice(32 * g, 32 * g + 32)
                            s = sc[b % 2][:, g, blk(j)]
                            go = j == 0 and not carried
                            mm(ps_num[r, blk(b)], vx[par][:, b, j * D + 32 * g:j * D + 32 * g + 32], s, start=go, stop=j == J - 1, skip_group_check=True)
                    for j in range(J):
                        for g in range(G):
                            r = slice(32 * g, 32 * g + 32)
                            s = sc[b % 2][:, g, blk(j)]
                            go = j == 0 and not carried
                            last = mm(ps_den[r, blk(b)], onesj[:, j, :], s, start=go, stop=j == J - 1, skip_group_check=True)
                    last.then_inc(a_nd, 1)

                def project(t):
                    pe.wait_ge(a_y, t + 1)
                    for b in range(NB):
                        last = mm(ps_b[:, blk(b)], yT[:, blk(b)], wo_sb[:], start=True, stop=True)
                    last.then_inc(a_o_ps, 1)

                pe.wait_ge(s_const, 1)
                pe.wait_ge(s_wqkv, 32)
                transposes(0)
                qk(0)
                vk(0)
                kv(0, 0)

                def body(t, par, prev, nxt):
                    scores(t, par, 0, not prev)
                    scores(t, par, 1, False)
                    num_den(t, par, 0, not prev)
                    if nxt:
                        pe.wait_ge(a_kv, t + 1)
                        transposes(t + 1)
                    scores(t, par, 2, False)
                    num_den(t, par, 1, not prev)
                    if nxt:
                        if prev:
                            pe.wait_ge(a_o, t - 1)
                        qk(t + 1)
                    scores(t, par, 3, False)
                    if nxt:
                        vk(t + 1)
                    num_den(t, par, 2, not prev)
                    if nxt:
                        kv(t + 1, 1 - par)
                    num_den(t, par, 3, not prev)
                    if prev:
                        project(t - 1)

                body(0, 0, False, True)
                body(1, 1, True, True)
                with pe.Fori(1, NT // 2 - 1) as q:
                    body(q * 2, 0, True, True)
                    body(q * 2 + 1, 1, True, True)
                body(NT - 2, 0, True, True)
                body(NT - 1, 1, True, False)
                project(NT - 1)

        s1 = sem("hidden_psum")
        gel = sem("gelu_done")
        hi = sem("hidden_high")
        lo = sem("hidden_rest")
        s2 = sem("second_done")
        yev = sem("y_read")
        yadd = sem("y_partly_summed")
        zfin = sem("y_summed")
        yT_ps, upd = sem("y_token_major_psum"), sem("u_updated")
        p_bn, p_mv, p_ve, p_rs, p_sd = (sem(f"p_{n}") for n in ("bn", "mv", "ve", "rstd", "std"))
        p_xh, p_xT_ps, p_xhi, p_xlo = (sem(f"p_{n}") for n in ("xhat", "xT_psum", "xT_high", "xT_rest"))
        p_lg_ps, p_nd, p_th, p_comb, p_sum = (sem(f"p_{n}") for n in ("logits_psum", "difference", "tanh", "comb", "combsum"))
        p_cT_ps, p_cT, p_cw, p_bc = (sem(f"p_{n}") for n in ("combT_psum", "combT", "comb_written", "comb_spread"))
        p_link = sem("p_router_chain")
        LINKS = 11
        c1h, c1, c2h, c2 = sem("w1_high"), sem("w1_split"), sem("w2_high"), sem("w2_split")
        f_bn, f_mv, f_ve, f_rs, f_n, f_o = (sem(f"f_{n}") for n in ("bn", "mv", "ve", "rstd", "norm", "sum"))
        f_out = [sem(f"f_out{n}") for n in range(2)]
        s_bias = sem("layer_bias")
        s_zero = sem("step_before_ready")

        comb_rows = nc.dram_tensor("comb_rows", [2, E * TILE], F32).ap()

        exp = ExitStack()
        with exp:
            def esb(name, shape, dt=F32):
                return sb(name, shape, dt, exp)

            def eps(name):
                return exp.enter_context(nc.psum_tensor(name, [P, 512], F32))

            w1h, w1l = esb("w1h", [P, E * F], F32R), esb("w1l", [P, E * F], F32R)
            w2h, w2l = esb("w2h", [P, E * FC * D], F32R), esb("w2l", [P, E * FC * D], F32R)
            hg = [esb(f"hg{n}", [P, TILE]) for n in range(HBUF)]
            hh = [esb(f"hh{n}", [P, TILE], F32R) for n in range(HBUF)]
            hl = [esb(f"hl{n}", [P, TILE], F32R) for n in range(HBUF)]
            xTh = [esb(f"xTh{n}", [P, TILE], F32R) for n in range(2)]
            xTl = [esb(f"xTl{n}", [P, TILE], F32R) for n in range(2)]
            xh = esb("xh", [P, TILE])
            bn, mv = esb("pbn", [P, NB, 6]), esb("pmv", [P, NB, 2])
            ve, rs, sd = esb("pve", [P, NB]), esb("prs", [P, NB]), esb("psd", [P, NB])
            fbn, fmv = esb("fbn", [P, NB, 6]), esb("fmv", [P, NB, 2])
            fve, frs = esb("fve", [P, NB]), esb("frs", [P, NB])
            fn, fo = esb("fn", [P, TILE]), [esb(f"fo{n}", [P, TILE]) for n in range(2)]
            lg, t1, t2, t3, lgf = (esb(n, [P, NB, E]) for n in ("lg", "t1", "t2", "t3", "lgf"))
            dd, cc = esb("dd", [P, NB, E, E]), esb("cc", [P, NB, E, E])
            rank, first, top2, nb_, qq, mm_ = (esb(n, [P, NB, E]) for n in ("rank", "first", "top2", "nb", "qq", "mm"))
            ndiff, th = esb("ndiff", [P, NB]), esb("th", [P, NB])
            comb = esb("comb", [P, E, NB])
            csum = [esb(f"csum{n}", [P, NB]) for n in range(2)]
            combT = esb("combT", [E * NB, P])
            cb = [esb(f"cb{n}", [P, E, TILE]) for n in range(2)]
            z, acc = esb("z", [P, TILE]), esb("acc", [P, TILE])
            b1c = esb("b1c", [P, K])
            ps_h = [eps(f"ps_h{n}") for n in range(HBUF)]
            ps_y = [eps(f"ps_y{n}") for n in range(2)]
            ps_t = eps("ps_t")
            ps_r = eps("ps_r")
            LG, CT = slice(0, NB * 2 * E), slice(128, 256)

            block = exp.enter_context(nc.Block())

            def steps(eng, step):
                with eng.Fori(0, L - 1) as l:
                    with eng.Fori(0, NT // 2 - 1) as q:
                        step(l, q * 2, 0)
                        step(l, q * 2 + 1, 1)
                    step(l, NT - 2, 0)
                    step(l, NT - 1, 1, end=True)
                step(L - 1, 0, 0)
                step(L - 1, 1, 1, fin=True)
                with eng.Fori(1, NT // 2 - 1) as q:
                    step(L - 1, q * 2, 0, fin=True)
                    step(L - 1, q * 2 + 1, 1, fin=True)
                step(L - 1, NT - 2, 0, fin=True)
                step(L - 1, NT - 1, 1, fin=True, nxt=False)

            @block.sync
            def _(sp):
                def spread(n, par):
                    sp.wait_ge(p_cT, n + 1)
                    sp.dma_start(comb_rows[par].rearrange("(r p) -> r p", p=P), combT[:]).then_inc(p_cw, 16)
                    sp.wait_ge(p_cw, n * 16 + 16)
                    sp.wait_ge(zfin, n)
                    sp.dma_start(cb[par][:].rearrange("p e n -> p (e n)"), comb_rows[par].partition_broadcast(P)).then_inc(p_bc, 16)

                def step(l, t, par, end=False, fin=False, nxt=True):
                    i = l * NT + t
                    if end:
                        sp.wait_ge(c2, l * E + E)
                        for e in range(E):
                            sp.dma_start(blocks(w2s[:, e * F:(e + 1) * F]),
                                         w2[ds(l + 1, 1), e].rearrange("o (c p) h -> p (o c) h", p=P)).then_inc(s_w2, 16)
                    if nxt:
                        spread(i + 1, 1 - par)
                    if fin:
                        sp.wait_ge(f_o, t)
                        sp.dma_start(out_t[ds(t - 1, 1)].rearrange("o p b d -> p (o b) d"), blocks(fo[1 - par][:])).then_inc(f_out[1 - par], 16)

                sp.sem_inc(f_out[0], 16)
                sp.sem_inc(f_out[1], 16)
                sp.wait_ge(s_zero, 1)
                spread(0, 0)
                steps(sp, step)
                sp.wait_ge(f_o, NT)
                sp.dma_start(out_t[NT - 1], blocks(fo[1][:])).then_inc(f_out[1], 16)
                sp.wait_ge(f_out[0], NT // 2 * 16 + 16)
                sp.wait_ge(f_out[1], NT // 2 * 16 + 16)

            @block.gpsimd
            def _(pool):
                g = nc.gpsimd
                def prepare(n):
                    pool.wait_ge(p_mv, n + 1)
                    g.tensor_tensor(ve[:], mv[:, :, 1], epsc[:], ALU.add).then_inc(p_ve, 1)
                    pool.wait_ge(p_ve, n + 1)
                    g.tensor_tensor(rs[:], ve[:], half[:], ALU.pow).then_inc(p_rs, 1)
                    pool.wait_ge(p_rs, n + 1)
                    g.tensor_tensor(sd[:], ve[:], rs[:], ALU.mult).then_inc(p_sd, 1)

                def finish(t):
                    pool.wait_ge(f_mv, t + 1)
                    g.tensor_tensor(fve[:], fmv[:, :, 1], epsc[:], ALU.add).then_inc(f_ve, 1)
                    pool.wait_ge(f_ve, t + 1)
                    g.tensor_tensor(frs[:], fve[:], half[:], ALU.pow).then_inc(f_rs, 1)

                def step(l, t, par, end=False, fin=False, nxt=True):
                    i = l * NT + t
                    if nxt:
                        prepare(i + 1)
                    if fin:
                        finish(t - 1)

                prepare(0)
                steps(pool, step)
                finish(NT - 1)

            @block.scalar
            def _(act):
                a = nc.scalar

                def gelu(l, i, k):
                    n = k % HBUF
                    act.wait_ge(s1, i * K + k + 1)
                    act.wait_ge(lo, i * K + k + 1)
                    a.activation(hg[n][:], ps_h[n][:], ACT.Gelu, bias=b1c[:, k:k + 1]).then_inc(gel, 1)

                def layer_bias(l):
                    a.activation(b1c[:], b1f[:, ds(l * K, K)], ACT.Identity).then_inc(s_bias, 1)
                    act.wait_ge(s_bias, l + 1)

                def high(i, k):
                    n = k % HBUF
                    act.wait_ge(gel, i * K + k + 1 + HBUF)
                    act.wait_ge(s2, i * K + k + 1)
                    a.activation(hh[n][:], hg[n][:], ACT.Identity).then_inc(hi, 1)

                def prep_x(n, par):
                    act.wait_ge(p_xT_ps, n + 1)
                    a.activation(xTh[par][:], ps_t[:], ACT.Identity).then_inc(p_xhi, 1)

                def prep_tanh(n):
                    act.wait_ge(p_nd, n + 1)
                    a.activation(th[:], ndiff[:], ACT.Tanh, scale=-0.5).then_inc(p_th, 1)

                def prep_combT(n):
                    act.wait_ge(p_cT_ps, n + 1)
                    if not isinstance(n, int) or n > 0:
                        act.wait_ge(p_cw, n * 16)
                    a.activation(combT[:], ps_r[0:E * NB, CT], ACT.Identity).then_inc(p_cT, 1)

                def split_w1(l, e):
                    a.activation(w1h[:, e * F:(e + 1) * F], w1s[:, ds(l * (E * F) + e * F, F)], ACT.Identity).then_inc(c1h, 1)

                def split_w2(l, e):
                    a.activation(w2h[:, e * F:(e + 1) * F], w2s[:, e * F:(e + 1) * F], ACT.Identity).then_inc(c2h, 1)

                def step(l, t, par, end=False, fin=False, nxt=True):
                    i = l * NT + t
                    for k in range(K):
                        if k < K - 1:
                            gelu(l, i, k + 1)
                        elif nxt:
                            if end:
                                act.wait_ge(gel, i * K + K + HBUF).then_inc(s_alone, 1)
                                layer_bias(l + 1)
                            gelu(l + 1 if end else l, i + 1, 0)
                        high(i, k)
                        if nxt and k == 8:
                            prep_x(i + 1, 1 - par)
                        if nxt and k == 13:
                            prep_tanh(i + 1)
                        if nxt and k == 15:
                            prep_combT(i + 1)
                        if end and k % FC == 1:
                            e = k // FC
                            act.wait_ge(s_w1g, L * E)
                            act.wait_ge(s1, i * K + (e + 1) * FC)
                            split_w1(l + 1, e)
                            if e:
                                if e == 1:
                                    act.wait_ge(s_w2, (l + 2) * (E * 16))
                                act.wait_ge(s2, i * K + e * FC + HBUF)
                                split_w2(l + 1, e - 1)
                    if end:
                        act.wait_ge(s2, i * K + K + HBUF)
                        split_w2(l + 1, E - 1)

                act.sem_inc(gel, HBUF)
                act.wait_ge(s_cols_ps, 1)
                a.activation(cols[:], ps_t[:, 0:112], ACT.Identity).then_inc(s_cols, 1)
                act.wait_ge(s_w2, E * 16)
                for e in range(E):
                    act.wait_ge(s_w1g, e + 1)
                    split_w1(0, e)
                    split_w2(0, e)
                prep_x(0, 0)
                prep_tanh(0)
                prep_combT(0)
                act.wait_ge(s_b1f, 1)
                layer_bias(0)
                gelu(0, 0, 0)
                steps(act, step)

            @block.vector
            def _(dve):
                v = nc.vector

                def rest(i, k):
                    n = k % HBUF
                    dve.wait_ge(hi, i * K + k + 1)
                    v.tensor_tensor(hl[n][:], hg[n][:], hh[n][:].bitcast(F32), ALU.subtract).then_inc(lo, 1)

                def combine(lcol, i, e, par):
                    dve.wait_ge(s2, i * K + (e + 1) * FC + HBUF)
                    if e == 0:
                        dve.wait_ge(p_bc, i * 16 + 16)
                        dve.wait_ge(yT_ps, i + 1)
                    v.scalar_tensor_tensor(acc[:] if e == 0 else z[:], ps_y[e % 2][:], cols[:, ds(lcol + e, 1)],
                                           cb[par][:, e, :], ALU.add, ALU.mult).then_inc(yev, 1)
                    if e:
                        dve.wait_ge(yev, i * E + e + 3)
                        dve.wait_ge(yadd, i * 2 + e)
                        v.tensor_tensor(acc[:], acc[:], z[:], ALU.add).then_inc(yadd, 1)

                def update(l, i, tp, par):
                    dve.wait_ge(yT_ps, i + 1)
                    for b in range(NB):
                        ub = u[:, ds(tp * TILE + b * P, P)]
                        last = v.scalar_tensor_tensor(ub, ub, csum[par][:, b:b + 1], ps_t[:, b * P:(b + 1) * P], ALU.mult, ALU.add)
                    last.then_inc(upd, 1)

                def prep_stats(t, n):
                    for b in range(NB):
                        last = v.bn_stats(bn[:, b, :], u[:, ds(t * TILE + b * P, P)])
                    last.then_inc(p_bn, 1)

                def prep_aggr(n):
                    dve.wait_ge(p_bn, n + 1).then_inc(s_alone, 1)
                    for b in range(NB):
                        last = v.bn_aggr(mv[:, b, :], bn[:, b, :])
                    last.then_inc(p_mv, 1)

                def prep_norm(t, n):
                    dve.wait_ge(p_rs, n + 1)
                    for b in range(NB):
                        last = v.tensor_scalar(xh[:, b * P:(b + 1) * P], u[:, ds(t * TILE + b * P, P)], mv[:, b, 0:1],
                                               rs[:, b:b + 1], ALU.subtract, ALU.mult)
                    last.then_inc(p_xh, 1)

                def prep_rest(n, par):
                    dve.wait_ge(p_xhi, n + 1)
                    v.tensor_tensor(xTl[par][:], ps_t[:], xTh[par][:].bitcast(F32), ALU.subtract).then_inc(p_xlo, 1)

                def over_blocks(ap):
                    return ap.unsqueeze(1).to_broadcast([P, NB, E])

                def over_experts(ap):
                    return ap.unsqueeze(2).to_broadcast([P, NB, E])

                def link(n, k):
                    dve.wait_ge(p_link, n * LINKS + k)

                def router1(l, n):
                    dve.wait_ge(p_lg_ps, n + 1)
                    dve.wait_ge(p_sd, n + 1)
                    v.reduce_sum(lg[:], ps_r[:, LG].rearrange("p (b h e) -> p b e h", b=NB, h=2), axis=AX.X).then_inc(p_link, 1)
                    v.tensor_tensor(t2[:], mv[:, :, 0:1].to_broadcast([P, NB, E]), over_blocks(cs[:, ds(l * E, E)]), ALU.mult)
                    link(n, 1)
                    v.tensor_tensor(t1[:], lg[:], over_experts(sd[:]), ALU.mult).then_inc(p_link, 1)
                    link(n, 2)
                    v.tensor_tensor(t3[:], t1[:], t2[:], ALU.add).then_inc(p_link, 1)
                    link(n, 3)
                    v.tensor_tensor(lgf[:], t3[:], over_blocks(rb[:, ds(l * E, E)]), ALU.add).then_inc(p_link, 1)

                def router2(n):
                    link(n, 4)
                    v.tensor_tensor(dd[:], lgf[:].unsqueeze(2).to_broadcast([P, NB, E, E]),
                                    lgf[:].unsqueeze(3).to_broadcast([P, NB, E, E]), ALU.subtract).then_inc(p_link, 1)
                    link(n, 5)
                    v.tensor_tensor(cc[:].rearrange("p b e f -> p b (e f)"), dd[:].rearrange("p b e f -> p b (e f)"),
                                    order[:].unsqueeze(1).to_broadcast([P, NB, E * E]), ALU.is_ge).then_inc(p_link, 1)
                    link(n, 6)
                    v.reduce_sum(rank[:], cc[:], axis=AX.X).then_inc(p_link, 1)
                    link(n, 7)
                    v.tensor_scalar(first[:], rank[:], 0.0, None, ALU.is_equal)
                    v.tensor_scalar(top2[:], rank[:], 2.0, 0.5, ALU.is_lt, ALU.mult).then_inc(p_link, 1)

                def router3(n):
                    link(n, 8)
                    v.scalar_tensor_tensor(nb_[:], rank[:], 1.0, first[:], ALU.is_equal, ALU.subtract).then_inc(p_link, 1)
                    link(n, 9)
                    v.tensor_tensor(qq[:], nb_[:], lgf[:], ALU.mult).then_inc(p_link, 1)
                    link(n, 10)
                    v.reduce_sum(ndiff[:], qq[:], axis=AX.X).then_inc(p_nd, 1)

                def router4(n, par):
                    dve.wait_ge(p_th, n + 1)
                    v.scalar_tensor_tensor(mm_[:], nb_[:], -0.5, over_experts(th[:]), ALU.mult, ALU.mult).then_inc(p_link, 1)
                    link(n, 11)
                    v.tensor_tensor(comb[:].rearrange("p e b -> p b e"), mm_[:], top2[:], ALU.add).then_inc(p_comb, 1)
                    dve.wait_ge(p_comb, n + 1)
                    v.reduce_sum(csum[par][:], comb[:].rearrange("p e b -> p b e"), axis=AX.X).then_inc(p_sum, 1)

                def rest_w1(l, e, n):
                    dve.wait_ge(c1h, n)
                    v.tensor_tensor(w1l[:, e * F:(e + 1) * F], w1s[:, ds(l * (E * F) + e * F, F)],
                                    w1h[:, e * F:(e + 1) * F].bitcast(F32), ALU.subtract).then_inc(c1, 1)

                def rest_w2(e, n):
                    dve.wait_ge(c2h, n)
                    v.tensor_tensor(w2l[:, e * F:(e + 1) * F], w2s[:, e * F:(e + 1) * F],
                                    w2h[:, e * F:(e + 1) * F].bitcast(F32), ALU.subtract).then_inc(c2, 1)

                def finish_stats(t, i):
                    dve.wait_ge(upd, i + 1).then_inc(s_alone, 1)
                    for b in range(NB):
                        last = v.bn_stats(fbn[:, b, :], u[:, ds(t * TILE + b * P, P)])
                    last.then_inc(f_bn, 1)
                    dve.wait_ge(f_bn, t + 1).then_inc(s_alone, 1)
                    for b in range(NB):
                        last = v.bn_aggr(fmv[:, b, :], fbn[:, b, :])
                    last.then_inc(f_mv, 1)

                def finish_sum(t, par):
                    dve.wait_ge(f_rs, t + 1)
                    for b in range(NB):
                        last = v.tensor_scalar(fn[:, b * P:(b + 1) * P], u[:, ds(t * TILE + b * P, P)], fmv[:, b, 0:1],
                                               frs[:, b:b + 1], ALU.subtract, ALU.mult)
                    last.then_inc(f_n, 1)
                    dve.wait_ge(f_n, t + 1)
                    dve.wait_ge(f_out[par], t // 2 * 16 + 16)
                    v.tensor_tensor(fo[par][:], fn[:], x1[:, ds(t * TILE, TILE)], ALU.add).then_inc(f_o, 1)

                def step(l, t, par, end=False, fin=False, nxt=True):
                    i = l * NT + t
                    tp = (i + NT - 1) % NT
                    bcol = (i + NT - 1) // NT * E + B2 - E
                    tn, ln = (0, l + 1) if end else (t + 1, l)
                    for k in range(K):
                        rest(i, k)
                        if k == 1:
                            combine_last(bcol, i, 1 - par)
                        if k == 4:
                            update(l, i, tp, 1 - par)
                        if k in (5, 9, 13):
                            combine(l * E + B2, i, k // FC - 1, par)
                        if fin and k == 6:
                            finish_stats(t - 1, i)
                        if fin and k == 9:
                            finish_sum(t - 1, 1 - par)
                        if nxt:
                            if k == 2:
                                prep_stats(tn, i + 1)
                            if k == 3:
                                prep_aggr(i + 1)
                            if k == 6:
                                prep_norm(tn, i + 1)
                            if k == 8:
                                prep_rest(i + 1, 1 - par)
                            if k == 11:
                                router1(ln, i + 1)
                            if k == 12:
                                router2(i + 1)
                            if k == 13:
                                router3(i + 1)
                            if k == 14:
                                router4(i + 1, 1 - par)
                        if end and k % FC == 1:
                            e = k // FC
                            rest_w1(l + 1, e, l * E + E + e + 1)
                            if e:
                                rest_w2(e - 1, l * E + E + e)
                    if end:
                        rest_w2(E - 1, l * E + 2 * E)

                def combine_last(bcol, i, par):
                    dve.wait_ge(s2, i * K + HBUF)
                    v.scalar_tensor_tensor(z[:], ps_y[1][:], cols[:, ds(bcol + E - 1, 1)], cb[par][:, E - 1, :],
                                           ALU.add, ALU.mult).then_inc(yev, 1)
                    dve.wait_ge(yev, i * E + 2)
                    dve.wait_ge(yadd, i * 2 + 1)
                    v.tensor_tensor(acc[:], acc[:], z[:], ALU.add).then_inc(zfin, 1)

                dve.sem_inc(lo, HBUF)
                dve.sem_inc(yev, 1)
                dve.sem_inc(yadd, 1)
                dve.wait_ge(s_small, 6 * 16)
                rwv = rw[:].rearrange("p (l e) -> p l e", l=L)
                rpv = rwp[:].rearrange("p (l h e) -> p l h e", l=L, h=2)
                v.tensor_copy(rpv[:, :, 0, :], rwv).then_inc(s_whi, 1)
                dve.wait_ge(s_whi, 1)
                v.tensor_tensor(rpv[:, :, 1, :], rwv, rpv[:, :, 0, :].bitcast(F32), ALU.subtract).then_inc(s_rwp, 1)
                v.memset(acc[:], 0.0)
                v.memset(cb[1][:, E - 1, :], 0.0)
                v.memset(csum[1][:], 1.0)
                v.memset(ps_y[1][:], 0.0).then_inc(s_zero, 1)
                dve.wait_ge(s_b1_ps, 1)
                v.tensor_copy(cs[:], ps_r[:, 64:80])
                v.tensor_tensor(b1f[:], ps_r[:, 0:64], cols[:, 0:64], ALU.add).then_inc(s_b1f, 1)
                for n in range(L * E):
                    w = w1s[:, n * F:(n + 1) * F]
                    v.tensor_scalar(w, w, cols[:, LNG + n:LNG + n + 1], None, ALU.mult).then_inc(s_w1g, 1)
                prep_stats(0, 0)
                prep_aggr(0)
                for e in range(E):
                    rest_w1(0, e, e + 1)
                    rest_w2(e, e + 1)
                prep_norm(0, 0)
                prep_rest(0, 0)
                router1(0, 0)
                router2(0)
                router3(0)
                router4(0, 0)
                steps(dve, step)
                i = L * NT
                combine_last((L - 1) * E + B2, i, 1)
                update(L, i, NT - 1, 1)
                finish_stats(NT - 1, i)
                finish_sum(NT - 1, 1)

            @block.tensor
            def _(pe):
                mm = nc.tensor.matmul

                def blk(b):
                    return slice(b * P, (b + 1) * P)

                def first(i, k, par):
                    n = k % HBUF
                    if k == 0:
                        pe.wait_ge(p_xlo, i + 1)
                    pe.wait_ge(gel, i * K + k + 1)
                    c = slice(k * P, (k + 1) * P)
                    mm(ps_h[n][:], w1h[:, c], xTh[par][:], start=True, stop=False)
                    mm(ps_h[n][:], w1h[:, c], xTl[par][:], start=False, stop=False)
                    mm(ps_h[n][:], w1l[:, c], xTh[par][:], start=False, stop=True).then_inc(s1, 1)

                def second(i, k):
                    n, e = k % HBUF, k // FC
                    if k % FC == 0:
                        pe.wait_ge(yev, i * E + e + 1)
                    pe.wait_ge(lo, i * K + k + 1 + HBUF)
                    c = slice(k * P, (k + 1) * P)
                    y = ps_y[e % 2]
                    mm(y[:], w2h[:, c], hh[n][:], start=k % FC == 0, stop=False)
                    mm(y[:], w2h[:, c], hl[n][:], start=False, stop=False)
                    mm(y[:], w2l[:, c], hh[n][:], start=False, stop=k % FC == FC - 1).then_inc(s2, 1)

                def y_tokens(i):
                    pe.wait_ge(zfin, i + 1)
                    for b in range(NB):
                        last = nc.tensor.transpose(ps_t[:, blk(b)], acc[:, blk(b)], ident[:])
                    last.then_inc(yT_ps, 1)

                def prep_x(n):
                    pe.wait_ge(p_xh, n + 1)
                    for b in range(NB):
                        last = nc.tensor.transpose(ps_t[:, blk(b)], xh[:, blk(b)], ident[:])
                    last.then_inc(p_xT_ps, 1)

                def prep_logits(l, n, par):
                    pe.wait_ge(p_xlo, n + 1)
                    if not isinstance(n, int) or n > 0:
                        pe.wait_ge(p_cT, n)
                    w = rwp[:, ds(l * 2 * E, 2 * E)]
                    for b in range(NB):
                        o = ps_r[:, b * 2 * E:(b + 1) * 2 * E]
                        mm(o, xTh[par][:, blk(b)], w, start=True, stop=False)
                        last = mm(o, xTl[par][:, blk(b)], w, start=False, stop=True)
                    last.then_inc(p_lg_ps, 1)

                def prep_combT(n):
                    pe.wait_ge(p_comb, n + 1)
                    nc.tensor.transpose(ps_r[0:E * NB, CT], comb[:].rearrange("p e b -> p (e b)"), ident[:]).then_inc(p_cT_ps, 1)

                def step(l, t, par, end=False, fin=False, nxt=True):
                    i = l * NT + t
                    ln = l + 1 if end else l
                    pe.wait_ge(c1, l * E + E)
                    pe.wait_ge(c2, l * E + E - 1)
                    for k in range(K):
                        if k < K - LEAD:
                            first(i, k + LEAD, par)
                        elif nxt:
                            if end and k == K - LEAD:
                                pe.wait_ge(c1, l * E + E + 1)
                            first(i + 1, k + LEAD - K, 1 - par)
                        if k == K - FC:
                            pe.wait_ge(c2, l * E + E)
                        second(i, k)
                        if k == 3:
                            y_tokens(i)
                        if nxt:
                            if k == 7:
                                pe.wait_ge(upd, i + 1)
                                prep_x(i + 1)
                            if k == 10:
                                prep_logits(ln, i + 1, 1 - par)
                            if k == 15:
                                prep_combT(i + 1)

                pe.sem_inc(s2, HBUF)
                pe.wait_ge(s_small, 6 * 16)
                nc.tensor.transpose(ps_t[:, 0:112], rows[:], ident[0:112, 0:112]).then_inc(s_cols_ps, 1)
                pe.wait_ge(s_cols, 1)
                pe.wait_ge(s_w1, L * 16)
                for n in range(L * E):
                    for c in range(FC):
                        mm(ps_r[:, n * FC + c:n * FC + c + 1], w1s[:, n * F + c * P:n * F + (c + 1) * P],
                           cols[:, LNB + n:LNB + n + 1], start=True, stop=True)
                mm(ps_r[:, 64:80], onesf[:], rw[:], start=True, stop=True).then_inc(s_b1_ps, 1)
                prep_x(0)
                pe.wait_ge(s_b1f, 1)
                prep_logits(0, 0, 0)
                prep_combT(0)
                pe.wait_ge(c1, 1)
                for k in range(LEAD):
                    first(0, k, 0)
                steps(pe, step)
                y_tokens(L * NT)


_INS = ['L0_attn_x', 'L0_attn_wqkv', 'L0_attn_wo', 'L0_ffn_router_w', 'L0_ffn_router_b', 'L0_ffn_ln_g', 'L0_ffn_ln_b',
        'L0_ffn_w1', 'L0_ffn_b1', 'L0_ffn_w2', 'L0_ffn_b2']
_OUT = (BATCH, SEQ, D)


def kernel(**inputs):
    import numpy as _np
    import concourse.bacc as _bacc
    from concourse import mybir as _mybir
    from concourse.bass_utils import run_bass_kernel_spmd as _run

    nc = _bacc.Bacc("TRN2", target_bir_lowering=False, num_devices=1)
    arrays, args = {}, []
    for name in _INS:
        a = _np.ascontiguousarray(inputs[name])
        arrays[f"in_{name}_dram"] = a
        args.append(nc.dram_tensor(f"in_{name}_dram", a.shape, _mybir.dt.from_np(a.dtype), kind="ExternalInput").ap())
    args.append(nc.dram_tensor("out_0_dram", _OUT, F32, kind="ExternalOutput").ap())
    sandwich_kernel(nc, *args)
    r = _run(nc, [arrays], core_ids=[0])
    return r.results[0]["out_0_dram"]
```

```python
import concourse.bass as bass
from concourse import mybir
from contextlib import ExitStack

F32 = mybir.dt.float32
F32R = mybir.dt.float32r
ALU = mybir.AluOpType
ACT = mybir.ActivationFunctionType
AX = mybir.AxisListType
ds = bass.ds

P = 128
BATCH, SEQ, D = 32, 256, 128
TOKENS = BATCH * SEQ
TILE = 512
NT = TOKENS // TILE
NB = TILE // P
HEADS, HD = 16, 8
G = 4
J = HEADS // G
L, E, F, FC = 4, 4, 512, 4
K = E * FC
EPS = 1e-5
TINY, NEVER = 1.2e-38, 3.0e38
BANKS = 4
PAIRS = 4
LEAD = 2 * PAIRS


def sandwich_kernel(nc, x, wqkv, wo, router_w, router_b, ln_g, ln_b, w1, b1, w2, b2, out):
    ctx = ExitStack()
    with ctx:
        def sb(name, shape, dt=F32, to=ctx):
            return to.enter_context(nc.sbuf_tensor(name, shape, dt))

        def sem(name):
            return ctx.enter_context(nc.semaphore(name))

        x1 = sb("x1", [P, NT * TILE])
        u = sb("u", [P, NT * TILE])
        w1s = sb("w1s", [P, E * F])
        w2s = sb("w2s", [P, E * FC * D])
        ident = sb("ident", [P, P])
        rows = sb("rows", [112, P])
        cols = sb("cols", [P, 112])
        b1f = sb("b1f", [P, L * K])
        rw = sb("rw", [P, L * E])
        rwp = sb("rwp", [P, L * 2 * E], F32R)
        cs = sb("cs", [P, L * E])
        rb = sb("rb", [P, L * E])
        onesf = sb("onesf", [P, P])
        order = sb("order", [P, E * E])
        half = sb("half", [P, NB])
        epsc = sb("epsc", [P, NB])
        LNG, LNB, B2 = 64, 80, 96

        s_wqkv, s_small, s_w1, s_w2 = sem("wqkv_in"), sem("small_in"), sem("w1_in"), sem("w2_in")
        s_pool0, s_pool1, s_pool2 = sem("pool_memset"), sem("pool_select"), sem("pool_bd")
        s_const = sem("constants_done")
        s_cols_ps, s_cols, s_b1_ps, s_b1f = sem("cols_psum"), sem("cols_ready"), sem("b1_psum"), sem("b1f_ready")
        s_whi, s_w1all = sem("router_high"), sem("w1_all_in")
        s_rwp = sem("router_split")
        s_alone = sem("wait_alone")
        s_x = sem("x_in")
        a_bn, a_mv, a_rs, a_ve, a_xn = sem("a_bn"), sem("a_mv"), sem("a_rstd"), sem("a_ve"), sem("a_xn")
        a_xT_ps, a_xT = sem("a_xT_psum"), sem("a_xT")
        a_q_ps, a_k_ps, a_v_ps, a_kt_ps, a_kv_ps = (sem(f"a_{n}_psum") for n in ("q", "k", "v", "kt", "kv"))
        a_q, a_k, a_v, a_kt, a_kv = (sem(f"a_{n}") for n in ("q", "k", "v", "kt", "kv"))
        a_s_ps, a_s = sem("a_scores_psum"), sem("a_scores")
        a_nd = sem("a_num_den_psum")
        a_den, a_rec, a_y = sem("a_den"), sem("a_rec"), sem("a_y")
        a_o_ps, a_o = sem("a_o_psum"), sem("a_o")
        a_lno = sem("a_ln_o")
        a_x1 = sem("a_x1")
        a_u = sem("a_u")

        x_t = x.rearrange("(t s) n d -> t (s n) d", t=NT)
        x_t = x_t.rearrange("t (b p) d -> t p b d", p=P)
        out_t = out.rearrange("(t s) n d -> t (s n) d", t=NT).rearrange("t (b p) d -> t p b d", p=P)

        def blocks(ap):
            return ap.rearrange("p (b n) -> p b n", b=NB)

        att = ExitStack()
        with att:
            def asb(name, shape, dt=F32):
                return sb(name, shape, dt, att)

            def aps(name):
                return att.enter_context(nc.psum_tensor(name, [P, 512], F32))

            wqkv_sb, wo_sb = asb("wqkv_sb", [P, 3 * D]), asb("wo_sb", [P, D])
            causal = asb("causal", [P, P])
            headbd = asb("headbd", [P, P])
            jmask = asb("jmask", [P, J])
            onesj = asb("onesj", [P, J, 32])
            bn = asb("bn", [P, NB, 6])
            mv = asb("mv", [P, NB, 2])
            ve, rs = asb("ve", [P, NB]), asb("rs", [P, NB])
            xn = asb("xn", [P, TILE])
            xnT = asb("xnT", [P, TILE])
            qT = [asb(f"qT{i}", [P, TILE]) for i in range(2)]
            kT = [asb(f"kT{i}", [P, TILE]) for i in range(2)]
            qx = [asb(f"qx{i}", [P, J, TILE]) for i in range(2)]
            VX = J * (D + HD)
            vx = [asb(f"vx{i}", [P, NB, VX]) for i in range(2)]
            ksum = asb("ksum", [P, 2])
            ktok = asb("ktok", [P, 2, D])
            kvbd = [asb(f"kvbd{i}", [P, 2, D]) for i in range(2)]
            ksbd = [asb(f"ksbd{i}", [P, 2, D]) for i in range(2)]
            sc = [asb(f"sc{i}", [P, G, J * P]) for i in range(2)]
            w1all = asb("w1all", [P, L * E * F])
            den, rec, yT = asb("den", [P, TILE]), asb("rec", [P, TILE]), asb("yT", [P, TILE])
            on = asb("on", [P, TILE])
            ps_s = [aps(f"ps_s{g}") for g in range(G)]
            ps_num, ps_den, ps_a, ps_b = aps("ps_num"), aps("ps_den"), aps("ps_a"), aps("ps_b")

            def own_heads(buf, b):
                v = buf[:, b, :].rearrange("p (j n) -> p j n", j=J)[:, :, 0:D]
                return v.rearrange("p j (g x) -> p j g x", g=G)[:, :, :, 0:HD]

            block = att.enter_context(nc.Block())

            @block.sync
            def _(sp):
                sp.dma_start(blocks(x1[:, 0:TILE]), x_t[0]).then_inc(s_x, 16)
                sp.dma_start(wqkv_sb[:], wqkv).then_inc(s_wqkv, 16)
                sp.dma_start(wo_sb[:], wo).then_inc(s_wqkv, 16)
                with sp.Fori(1, NT) as t:
                    sp.wait_ge(s_x, t * 16)
                    sp.dma_start(blocks(x1[:, ds(t * TILE, TILE)]), x_t[ds(t, 1)].rearrange("o p b d -> p (o b) d")).then_inc(s_x, 16)
                sp.dma_start(rows[0:64, :], b1.rearrange("l e (c p) -> (l e c) p", p=P)).then_inc(s_small, 16)
                sp.dma_start(rows[LNG:LNG + 16, :], ln_g.rearrange("l e h -> (l e) h")).then_inc(s_small, 16)
                sp.dma_start(rows[LNB:LNB + 16, :], ln_b.rearrange("l e h -> (l e) h")).then_inc(s_small, 16)
                sp.dma_start(rows[B2:B2 + 16, :], b2.rearrange("l e h -> (l e) h")).then_inc(s_small, 16)
                sp.dma_start(rw[:].rearrange("h (l e) -> h l e", l=L), router_w.rearrange("l h e -> h l e")).then_inc(s_small, 16)
                sp.dma_start(rb[:], router_b.rearrange("l e -> (l e)").partition_broadcast(P)).then_inc(s_small, 16)
                for l in range(L):
                    sp.dma_start(w1all[:, l * E * F:(l + 1) * E * F].rearrange("h (e f) -> h e f", e=E),
                                 w1[l].rearrange("e h f -> h e f")).then_inc(s_w1all, 16)
                sp.dma_start(w1s[:].rearrange("h (e f) -> h e f", e=E), w1[0].rearrange("e h f -> h e f")).then_inc(s_w1, 16)
                for e in range(E):
                    sp.dma_start(blocks(w2s[:, e * F:(e + 1) * F]),
                                 w2[0, e].rearrange("(c p) h -> p c h", p=P)).then_inc(s_w2, 16)

            @block.gpsimd
            def _(pool):
                g = nc.gpsimd
                g.memset(ident[:], 0.0)
                g.memset(causal[:], 1.0)
                g.memset(headbd[:], 1.0)
                g.memset(onesj[:], 0.0)
                g.memset(half[:], -0.5)
                g.memset(epsc[:], EPS)
                g.memset(onesf[:], 1.0)
                g.memset(order[:], 0.0).then_inc(s_pool0, 1)
                pool.wait_ge(s_pool0, 1)
                g.affine_select(out=ident[:], in_=ident[:], compare_op=ALU.not_equal, fill=1.0, base=0,
                                pattern=[[-1, P]], channel_multiplier=1)
                g.affine_select(out=causal[:], in_=causal[:], compare_op=ALU.is_ge, fill=0.0, base=0,
                                pattern=[[1, P]], channel_multiplier=-1)
                g.affine_select(out=headbd[:], in_=headbd[:], compare_op=ALU.is_ge, fill=0.0, base=0,
                                pattern=[[-HD, HEADS], [0, HD]], channel_multiplier=1).then_inc(s_pool1, 1)
                for j in range(J):
                    g.memset(onesj[:, j, HD * j:HD * (j + 1)], 1.0)
                for e in range(E):
                    g.memset(order[:, e * E + e:e * E + e + 1], NEVER)
                    if e < E - 1:
                        g.memset(order[:, e * E + e + 1:(e + 1) * E], TINY)
                pool.wait_ge(s_pool1, 1)
                g.affine_select(out=headbd[:], in_=headbd[:], compare_op=ALU.is_ge, fill=0.0, base=HD - 1,
                                pattern=[[HD, HEADS], [0, HD]], channel_multiplier=-1).then_inc(s_const, 1)

                def rstd(n):
                    pool.wait_ge(a_mv, n + 1)
                    g.tensor_tensor(ve[:], mv[:, :, 1], epsc[:], ALU.add).then_inc(a_ve, 1)
                    pool.wait_ge(a_ve, n + 1)
                    g.tensor_tensor(rs[:], ve[:], half[:], ALU.pow).then_inc(a_rs, 1)

                with pool.Fori(0, 3 * NT) as n:
                    rstd(n)

            def layer_norm_stats(dve, src, n):
                for b in range(NB):
                    last = nc.vector.bn_stats(bn[:, b, :], src(b))
                last.then_inc(a_bn, 1)
                dve.wait_ge(a_bn, n + 1).then_inc(s_alone, 1)
                for b in range(NB):
                    last = nc.vector.bn_aggr(mv[:, b, :], bn[:, b, :])
                last.then_inc(a_mv, 1)
                dve.wait_ge(a_rs, n + 1)

            def normed(dst, src, b):
                return nc.vector.tensor_scalar(dst, src, mv[:, b, 0:1], rs[:, b:b + 1], ALU.subtract, ALU.mult)

            @block.vector
            def _(dve):
                v = nc.vector

                def norm_x(t, n):
                    dve.wait_ge(s_x, t * 16 + 16).then_inc(s_alone, 1)
                    layer_norm_stats(dve, lambda b: x1[:, ds(t * TILE + b * P, P)], n)
                    for b in range(NB):
                        last = normed(xn[:, b * P:(b + 1) * P], x1[:, ds(t * TILE + b * P, P)], b)
                    last.then_inc(a_xn, 1)

                def spread_v(t, par):
                    dve.wait_ge(a_v_ps, t + 1)
                    for b in range(NB):
                        last = v.tensor_copy(own_heads(vx[par], b), ps_b[:, b * P:(b + 1) * P].rearrange(
                            "p (g j e) -> p j g e", g=G, j=J))
                    last.then_inc(a_v, 1)

                def state(t, par):
                    dve.wait_ge(a_kv_ps, t + 1)
                    dve.wait_ge(a_k, t + 1)
                    v.tensor_tensor(kvbd[par][:], ps_a[:, 256:512].rearrange("p (s n) -> p s n", s=2),
                                    headbd[:].unsqueeze(1).to_broadcast([P, 2, P]), ALU.mult)
                    for s in range(2):
                        last = v.tensor_scalar(ksbd[par][:, s, :], headbd[:], ksum[:, s:s + 1], None, ALU.mult)
                    last.then_inc(a_kv, 1)

                def mask(t, b, fresh=False):
                    if not fresh:
                        dve.wait_ge(a_nd, t * NB + b - 1)
                    for g in range(G):
                        dve.wait_ge(a_s_ps, t * 16 + b * G + g + 1)
                        v.tensor_tensor(sc[b % 2][:, g, :].rearrange("p (j n) -> p j n", j=J),
                                        ps_s[g][:].rearrange("p (j n) -> p j n", j=J),
                                        causal[:].unsqueeze(1).to_broadcast([P, J, P]), ALU.mult).then_inc(a_s, 1)

                def divide(t):
                    dve.wait_ge(a_nd, t * NB + NB)
                    v.tensor_scalar(den[:], ps_den[:], EPS, None, ALU.add).then_inc(a_den, 1)
                    dve.wait_ge(a_den, t + 1)
                    v.reciprocal(rec[:], den[:]).then_inc(a_rec, 1)
                    dve.wait_ge(a_rec, t + 1)
                    v.tensor_tensor(yT[:], ps_num[:], rec[:], ALU.mult).then_inc(a_y, 1)

                def finish(t, n):
                    dve.wait_ge(a_o_ps, t + 1)
                    layer_norm_stats(dve, lambda b: ps_b[:, b * P:(b + 1) * P], n)
                    for b in range(NB):
                        last = normed(on[:, b * P:(b + 1) * P], ps_b[:, b * P:(b + 1) * P], b)
                    last.then_inc(a_o, 1)
                    dve.wait_ge(a_o, t + 1)
                    xt = x1[:, ds(t * TILE, TILE)]
                    v.tensor_tensor(xt, xt, on[:], ALU.add).then_inc(a_x1, 1)
                    dve.wait_ge(a_x1, t + 1).then_inc(s_alone, 1)
                    layer_norm_stats(dve, lambda b: x1[:, ds(t * TILE + b * P, P)], n + 1)
                    for b in range(NB):
                        last = normed(u[:, ds(t * TILE + b * P, P)], x1[:, ds(t * TILE + b * P, P)], b)
                    last.then_inc(a_u, 1)

                for par in range(2):
                    last = v.memset(vx[par][:], 0.0)
                dve.wait_ge(s_const, 1)
                v.reduce_sum(jmask[:], headbd[:].rearrange("p (g j e) -> p j g e", g=G, j=J)[:, :, :, 0], axis=AX.X).then_inc(s_pool2, 1)
                norm_x(0, 0)
                spread_v(0, 0)
                state(0, 0)

                def body(t, par, prev, nxt, n):
                    mask(t, 0, not prev)
                    if prev:
                        divide(t - 1)
                    if nxt:
                        norm_x(t + 1, n)
                    mask(t, 1, not prev)
                    mask(t, 2)
                    mask(t, 3)
                    if nxt:
                        spread_v(t + 1, 1 - par)
                        state(t + 1, 1 - par)
                    if prev:
                        finish(t - 1, n + (1 if nxt else 0))

                body(0, 0, False, True, 1)
                body(1, 1, True, True, 2)
                with dve.Fori(1, NT // 2 - 1) as q:
                    body(q * 2, 0, True, True, q * 6 - 1)
                    body(q * 2 + 1, 1, True, True, q * 6 + 2)
                body(NT - 2, 0, True, True, 3 * NT - 7)
                body(NT - 1, 1, True, False, 3 * NT - 4)
                divide(NT - 1)
                finish(NT - 1, 3 * NT - 2)
                dve.wait_ge(s_b1_ps, 1)
                v.tensor_copy(cs[:], ps_s[0][:, 64:80])
                v.tensor_tensor(b1f[:], ps_s[0][:, 0:64], cols[:, 0:64], ALU.add).then_inc(s_b1f, 1)

            @block.scalar
            def _(act):
                a = nc.scalar

                def evacuate(t, par):
                    act.wait_ge(a_xT_ps, t + 1)
                    a.activation(xnT[:], ps_a[:], ACT.Identity).then_inc(a_xT, 1)
                    act.wait_ge(a_q_ps, t + 1)
                    a.activation(qT[par][:], ps_b[:], ACT.Relu)
                    for j in range(J):
                        last = a.activation(qx[par][:, j, :], ps_b[:], ACT.Relu, scale=jmask[:, j:j + 1])
                    last.then_inc(a_q, 1)
                    act.wait_ge(a_k_ps, t + 1)
                    for s in range(2):
                        c = s * SEQ
                        a.activation(kT[par][:, c:c + P], ps_a[:, c:c + P], ACT.Relu, accum_out=ksum[:, s:s + 1])
                        last = a.activation(kT[par][:, c + P:c + 2 * P], ps_a[:, c + P:c + 2 * P], ACT.Relu)
                    last.then_inc(a_k, 1)
                    act.wait_ge(a_kt_ps, t + 1)
                    a.activation(ktok[:].rearrange("p s n -> p (s n)"), ps_a[:, 0:256], ACT.Relu).then_inc(a_kt, 1)

                act.wait_ge(s_pool2, 1)
                evacuate(0, 0)

                def body(t, par):
                    act.wait_ge(a_nd, t * NB)
                    evacuate(t + 1, 1 - par)

                evacuate(1, 1)
                with act.Fori(1, NT // 2) as q:
                    body(q * 2 - 1, 1)
                    body(q * 2, 0)
                act.wait_ge(s_cols_ps, 1)
                a.activation(cols[:], ps_a[:, 0:112], ACT.Identity).then_inc(s_cols, 1)

            @block.tensor
            def _(pe):
                mm = nc.tensor.matmul

                def blk(b):
                    return slice(b * P, (b + 1) * P)

                def transposes(t):
                    pe.wait_ge(a_xn, t + 1)
                    for b in range(NB):
                        last = nc.tensor.transpose(ps_a[:, blk(b)], xn[:, blk(b)], ident[:])
                    last.then_inc(a_xT_ps, 1)

                def qk(t):
                    pe.wait_ge(a_xT, t + 1)
                    mm(ps_b[:], wqkv_sb[:, 0:D], xnT[:], start=True, stop=True).then_inc(a_q_ps, 1)
                    mm(ps_a[:], wqkv_sb[:, D:2 * D], xnT[:], start=True, stop=True).then_inc(a_k_ps, 1)

                def vk(t):
                    pe.wait_ge(a_q, t + 1)
                    for b in range(NB):
                        last = mm(ps_b[:, blk(b)], xnT[:, blk(b)], wqkv_sb[:, 2 * D:3 * D], start=True, stop=True)
                    last.then_inc(a_v_ps, 1)
                    pe.wait_ge(a_k, t + 1)
                    for s in range(2):
                        last = mm(ps_a[:, blk(s)], xnT[:, blk(2 * s)], wqkv_sb[:, D:2 * D], start=True, stop=True)
                    last.then_inc(a_kt_ps, 1)

                def kv(t, par):
                    pe.wait_ge(a_kt, t + 1)
                    pe.wait_ge(a_v, t + 1)
                    for s in range(2):
                        moving = own_heads(vx[par], 2 * s).rearrange("p j g e -> p g j e")
                        last = mm(ps_a[:, 256 + s * P:256 + (s + 1) * P].rearrange("p (g j e) -> p g j e", g=G, j=J),
                                  ktok[:, s, :], moving, start=True, stop=True)
                    last.then_inc(a_kv_ps, 1)

                def scores(t, par, b, first):
                    for g in range(G):
                        r = slice(32 * g, 32 * g + 32)
                        if not first:
                            pe.wait_ge(a_s, t * 16 + b * G + g - G + 1)
                        mm(ps_s[g][:].rearrange("p (j n) -> p j n", j=J), kT[par][r, blk(b)], qx[par][r, :, blk(b)],
                           start=True, stop=True).then_inc(a_s_ps, 1)

                def num_den(t, par, b, first):
                    if not first and b == 0:
                        pe.wait_ge(a_y, t)
                    pe.wait_ge(a_s, t * 16 + b * G + G)
                    carried = b % 2
                    if carried:
                        pe.wait_ge(a_kv, t + 1)
                        for ps, st in ((ps_num, kvbd), (ps_den, ksbd)):
                            for g in range(G):
                                r = slice(32 * g, 32 * g + 32)
                                mm(ps[r, blk(b)], st[par][:, b // 2, r], qT[par][:, blk(b)], start=True, stop=False,
                                   skip_group_check=True)
                    for j in range(J):
                        for g in range(G):
                            r = slice(32 * g, 32 * g + 32)
                            s = sc[b % 2][:, g, blk(j)]
                            go = j == 0 and not carried
                            mm(ps_num[r, blk(b)], vx[par][:, b, j * D + 32 * g:j * D + 32 * g + 32], s, start=go, stop=j == J - 1, skip_group_check=True)
                    for j in range(J):
                        for g in range(G):
                            r = slice(32 * g, 32 * g + 32)
                            s = sc[b % 2][:, g, blk(j)]
                            go = j == 0 and not carried
                            last = mm(ps_den[r, blk(b)], onesj[:, j, :], s, start=go, stop=j == J - 1, skip_group_check=True)
                    last.then_inc(a_nd, 1)

                def project(t):
                    pe.wait_ge(a_y, t + 1)
                    for b in range(NB):
                        last = mm(ps_b[:, blk(b)], yT[:, blk(b)], wo_sb[:], start=True, stop=True)
                    last.then_inc(a_o_ps, 1)

                pe.wait_ge(s_const, 1)
                pe.wait_ge(s_wqkv, 32)
                transposes(0)
                qk(0)
                vk(0)
                kv(0, 0)

                def body(t, par, prev, nxt):
                    scores(t, par, 0, not prev)
                    scores(t, par, 1, False)
                    num_den(t, par, 0, not prev)
                    if nxt:
                        pe.wait_ge(a_kv, t + 1)
                        transposes(t + 1)
                    scores(t, par, 2, False)
                    num_den(t, par, 1, not prev)
                    if nxt:
                        if prev:
                            pe.wait_ge(a_o, t - 1)
                        qk(t + 1)
                    scores(t, par, 3, False)
                    if nxt:
                        vk(t + 1)
                    num_den(t, par, 2, not prev)
                    if nxt:
                        kv(t + 1, 1 - par)
                    num_den(t, par, 3, not prev)
                    if prev:
                        project(t - 1)

                body(0, 0, False, True)
                body(1, 1, True, True)
                with pe.Fori(1, NT // 2 - 1) as q:
                    body(q * 2, 0, True, True)
                    body(q * 2 + 1, 1, True, True)
                body(NT - 2, 0, True, True)
                body(NT - 1, 1, True, False)
                project(NT - 1)

                pe.wait_ge(s_small, 6 * 16)
                nc.tensor.transpose(ps_a[:, 0:112], rows[:], ident[0:112, 0:112]).then_inc(s_cols_ps, 1)
                pe.wait_ge(s_cols, 1)
                pe.wait_ge(s_w1all, L * 16)
                for n in range(L * E):
                    for c in range(FC):
                        mm(ps_s[0][:, n * FC + c:n * FC + c + 1], w1all[:, n * F + c * P:n * F + (c + 1) * P],
                           cols[:, LNB + n:LNB + n + 1], start=True, stop=True)
                mm(ps_s[0][:, 64:80], onesf[:], rw[:], start=True, stop=True).then_inc(s_b1_ps, 1)

        s1 = sem("hidden_psum")
        gel = sem("gelu_done")
        hi = sem("hidden_high")
        lo = sem("hidden_rest")
        s2 = sem("second_done")
        yev = sem("y_read")
        yadd = sem("y_partly_summed")
        zfin = sem("y_summed")
        yT_ps, upd = sem("y_token_major_psum"), sem("u_updated")
        p_bn, p_mv, p_ve, p_rs, p_sd = (sem(f"p_{n}") for n in ("bn", "mv", "ve", "rstd", "std"))
        p_xh, p_xT_ps, p_xhi, p_xlo = (sem(f"p_{n}") for n in ("xhat", "xT_psum", "xT_high", "xT_rest"))
        p_lg_ps, p_nd, p_th, p_comb, p_sum = (sem(f"p_{n}") for n in ("logits_psum", "difference", "tanh", "comb", "combsum"))
        p_cT_ps, p_cT, p_cw, p_bc = (sem(f"p_{n}") for n in ("combT_psum", "combT", "comb_written", "comb_spread"))
        p_link = sem("p_router_chain")
        LINKS = 11
        c1h, c1, c2h, c2 = sem("w1_high"), sem("w1_split"), sem("w2_high"), sem("w2_split")
        s_bias = sem("layer_bias")
        f_bn, f_mv, f_ve, f_rs, f_n, f_o = (sem(f"f_{n}") for n in ("bn", "mv", "ve", "rstd", "norm", "sum"))
        f_out = [sem(f"f_out{n}") for n in range(2)]
        s_zero = sem("step_before_ready")

        comb_rows = nc.dram_tensor("comb_rows", [2, E * TILE], F32).ap()

        exp = ExitStack()
        with exp:
            def esb(name, shape, dt=F32):
                return sb(name, shape, dt, exp)

            def eps(name):
                return exp.enter_context(nc.psum_tensor(name, [P, 512], F32))

            w1h, w1l = esb("w1h", [P, E * F], F32R), esb("w1l", [P, E * F], F32R)
            w2h, w2l = esb("w2h", [P, E * FC * D], F32R), esb("w2l", [P, E * FC * D], F32R)
            hg = [esb(f"hg{n}", [P, 2 * TILE]) for n in range(PAIRS)]
            hh = [esb(f"hh{n}", [P, 2 * TILE], F32R) for n in range(PAIRS)]
            hl = [esb(f"hl{n}", [P, 2 * TILE], F32R) for n in range(PAIRS)]
            xTh = [esb(f"xTh{n}", [P, TILE], F32R) for n in range(2)]
            xTl = [esb(f"xTl{n}", [P, TILE], F32R) for n in range(2)]
            xh = esb("xh", [P, TILE])
            bn, mv = esb("pbn", [P, NB, 6]), esb("pmv", [P, NB, 2])
            ve, rs, sd = esb("pve", [P, NB]), esb("prs", [P, NB]), esb("psd", [P, NB])
            fbn, fmv = esb("fbn", [P, NB, 6]), esb("fmv", [P, NB, 2])
            fve, frs = esb("fve", [P, NB]), esb("frs", [P, NB])
            fn, fo = esb("fn", [P, TILE]), [esb(f"fo{n}", [P, TILE]) for n in range(2)]
            lg, t1, t2, t3, lgf = (esb(n, [P, NB, E]) for n in ("lg", "t1", "t2", "t3", "lgf"))
            dd, cc = esb("dd", [P, NB, E, E]), esb("cc", [P, NB, E, E])
            rank, first, top2, second_first, signed, shift = (
                esb(n, [P, NB, E]) for n in ("rank", "first", "top2", "second_first", "signed", "shift"))
            ndiff, th = esb("ndiff", [P, NB]), esb("th", [P, NB])
            comb = esb("comb", [P, E, NB])
            csum = [esb(f"csum{n}", [P, NB]) for n in range(2)]
            combT = esb("combT", [E * NB, P])
            cb = [esb(f"cb{n}", [P, E, TILE]) for n in range(2)]
            z, acc = esb("z", [P, TILE]), [esb(f"acc{n}", [P, TILE]) for n in range(2)]
            b1c = esb("b1c", [P, K])
            ps_h = [eps(f"ps_h{n}") for n in range(BANKS)]
            ps_y = [eps(f"ps_y{n}") for n in range(2)]
            ps_t = eps("ps_t")
            ps_r = eps("ps_r")
            LG, CT = slice(0, NB * 2 * E), slice(128, 256)

            block = exp.enter_context(nc.Block())

            def steps(eng, step):
                def middle(l, **kw):
                    with eng.Fori(1, NT // 2 - 1) as q:
                        step(l, q * 2, 0, **kw)
                        step(l, q * 2 + 1, 1, **kw)

                with eng.Fori(0, L - 1) as l:
                    step(l, 0, 0, start=True)
                    step(l, 1, 1)
                    middle(l)
                    step(l, NT - 2, 0)
                    step(l, NT - 1, 1, end=True)
                step(L - 1, 0, 0, start=True)
                step(L - 1, 1, 1, fin=True)
                middle(L - 1, fin=True)
                step(L - 1, NT - 2, 0, fin=True)
                step(L - 1, NT - 1, 1, fin=True, nxt=False)

            @block.sync
            def _(sp):
                def spread(n, par):
                    sp.wait_ge(p_cT, n + 1)
                    sp.dma_start(comb_rows[par].rearrange("(r p) -> r p", p=P), combT[:]).then_inc(p_cw, 16)
                    sp.wait_ge(p_cw, n * 16 + 16)
                    sp.wait_ge(zfin, n)
                    sp.dma_start(cb[par][:].rearrange("p e n -> p (e n)"), comb_rows[par].partition_broadcast(P)).then_inc(p_bc, 16)

                def step(l, t, par, start=False, end=False, fin=False, nxt=True):
                    i = l * NT + t
                    if nxt:
                        spread(i + 1, 1 - par)
                    if start and not isinstance(l, int):
                        sp.wait_ge(c1, l * E + E)
                        sp.wait_ge(c2, l * E + E)
                        for e in range(E):
                            sp.dma_start(w1s[:, e * F:(e + 1) * F], w1[ds(l + 1, 1), e].rearrange("o h f -> (o h) f")).then_inc(s_w1, 16)
                            sp.dma_start(blocks(w2s[:, e * F:(e + 1) * F]),
                                         w2[ds(l + 1, 1), e].rearrange("o (c p) h -> p (o c) h", p=P)).then_inc(s_w2, 16)
                    if fin:
                        sp.wait_ge(f_o, t)
                        sp.dma_start(out_t[ds(t - 1, 1)].rearrange("o p b d -> p (o b) d"), blocks(fo[1 - par][:])).then_inc(f_out[1 - par], 16)

                sp.sem_inc(f_out[0], 16)
                sp.sem_inc(f_out[1], 16)
                sp.wait_ge(s_zero, 1)
                spread(0, 0)
                steps(sp, step)
                sp.wait_ge(f_o, NT)
                sp.dma_start(out_t[NT - 1], blocks(fo[1][:])).then_inc(f_out[1], 16)
                sp.wait_ge(f_out[0], NT // 2 * 16 + 16)
                sp.wait_ge(f_out[1], NT // 2 * 16 + 16)

            @block.gpsimd
            def _(pool):
                g = nc.gpsimd

                def prepare(n):
                    pool.wait_ge(p_mv, n + 1)
                    g.tensor_tensor(ve[:], mv[:, :, 1], epsc[:], ALU.add).then_inc(p_ve, 1)
                    pool.wait_ge(p_ve, n + 1)
                    g.tensor_tensor(rs[:], ve[:], half[:], ALU.pow).then_inc(p_rs, 1)
                    pool.wait_ge(p_rs, n + 1)
                    g.tensor_tensor(sd[:], ve[:], rs[:], ALU.mult).then_inc(p_sd, 1)

                def finish(t):
                    pool.wait_ge(f_mv, t + 1)
                    g.tensor_tensor(fve[:], fmv[:, :, 1], epsc[:], ALU.add).then_inc(f_ve, 1)
                    pool.wait_ge(f_ve, t + 1)
                    g.tensor_tensor(frs[:], fve[:], half[:], ALU.pow).then_inc(f_rs, 1)

                def step(l, t, par, start=False, end=False, fin=False, nxt=True):
                    i = l * NT + t
                    if nxt:
                        prepare(i + 1)
                    if fin:
                        finish(t - 1)

                prepare(0)
                steps(pool, step)
                finish(NT - 1)

            @block.scalar
            def _(act):
                a = nc.scalar

                def gelu(i, k):
                    act.wait_ge(s1, i * K + k + 1)
                    if k % 2 == 0:
                        act.wait_ge(lo, i * (K // 2) + k // 2 + 1)
                    a.activation(hg[k // 2 % PAIRS][:, k % 2 * TILE:(k % 2 + 1) * TILE], ps_h[k % BANKS][:], ACT.Gelu,
                                 bias=b1c[:, k:k + 1]).then_inc(gel, 1)

                def high(i, j):
                    act.wait_ge(gel, i * K + 2 * j + 2 + BANKS)
                    act.wait_ge(s2, i * (K // 2) + j + 1)
                    a.activation(hh[j % PAIRS][:], hg[j % PAIRS][:], ACT.Identity).then_inc(hi, 1)

                def prep_x(n, par):
                    act.wait_ge(p_xT_ps, n + 1)
                    a.activation(xTh[par][:], ps_t[:], ACT.Identity).then_inc(p_xhi, 1)

                def prep_tanh(n):
                    act.wait_ge(p_nd, n + 1)
                    a.activation(th[:], ndiff[:], ACT.Tanh, scale=-0.5).then_inc(p_th, 1)

                def prep_combT(n):
                    act.wait_ge(p_cT_ps, n + 1)
                    if not isinstance(n, int) or n > 0:
                        act.wait_ge(p_cw, n * 16)
                    a.activation(combT[:], ps_r[0:E * NB, CT], ACT.Identity).then_inc(p_cT, 1)

                def split_w1(l, e):
                    a.activation(w1h[:, e * F:(e + 1) * F], w1s[:, e * F:(e + 1) * F], ACT.Identity,
                                 scale=cols[:, ds(l * E + e + LNG, 1)]).then_inc(c1h, 1)

                def split_w2(e):
                    a.activation(w2h[:, e * F:(e + 1) * F], w2s[:, e * F:(e + 1) * F], ACT.Identity).then_inc(c2h, 1)

                def layer_bias(l):
                    a.activation(b1c[:], b1f[:, ds(l * K, K)], ACT.Identity).then_inc(s_bias, 1)
                    act.wait_ge(s_bias, l + 1)

                def step(l, t, par, start=False, end=False, fin=False, nxt=True):
                    i = l * NT + t
                    for j in range(K // 2):
                        high(i, j)
                        if j < K // 2 - 1:
                            gelu(i, 2 * j + 2)
                            gelu(i, 2 * j + 3)
                        elif nxt:
                            if end:
                                act.wait_ge(gel, i * K + K + BANKS).then_inc(s_alone, 1)
                                layer_bias(l + 1)
                            gelu(i + 1, 0)
                            gelu(i + 1, 1)
                        if nxt and j == 3:
                            prep_x(i + 1, 1 - par)
                        if nxt and j == 6:
                            prep_tanh(i + 1)
                        if nxt and j == 7:
                            prep_combT(i + 1)
                        if end and j % 2 == 1:
                            e = j // 2
                            if e == 0:
                                act.wait_ge(s_w1, (l + 1) * (E * 16) + 16)
                            act.wait_ge(s1, i * K + (e + 1) * FC).then_inc(s_alone, 1)
                            split_w1(l + 1, e)
                        if end and j in (5, 7):
                            e = (j - 5) // 2
                            if e == 0:
                                act.wait_ge(s_w2, (l + 2) * (E * 16))
                            act.wait_ge(s2, i * (K // 2) + 2 * e + 2 + PAIRS)
                            split_w2(e)
                        if start and j in (1, 3):
                            e = j // 2 + 2
                            act.wait_ge(s2, i * (K // 2) + j // 2 * 2 - 2 + PAIRS)
                            split_w2(e)

                act.sem_inc(gel, BANKS)
                act.wait_ge(s_w1, 16)
                act.wait_ge(s_w2, E * 16)
                for e in range(E):
                    split_w1(0, e)
                prep_x(0, 0)
                split_w2(0)
                split_w2(1)
                prep_tanh(0)
                prep_combT(0)
                layer_bias(0)
                gelu(0, 0)
                gelu(0, 1)
                steps(act, step)

            @block.vector
            def _(dve):
                v = nc.vector

                def rest(i, j):
                    dve.wait_ge(hi, i * (K // 2) + j + 1)
                    n = j % PAIRS
                    v.tensor_tensor(hl[n][:], hg[n][:], hh[n][:].bitcast(F32), ALU.subtract).then_inc(lo, 1)

                def combine(n, e, par, bcol, pairs, reads, adds):
                    dve.wait_ge(s2, pairs)
                    if e:
                        dve.wait_ge(zfin if e == 1 else yadd, adds)
                    if e == 0:
                        dve.wait_ge(p_bc, n * 16 + 16)
                    v.scalar_tensor_tensor(acc[par][:] if e == 0 else z[:], ps_y[e % 2][:], cols[:, ds(bcol + e, 1)],
                                           cb[par][:, e, :], ALU.add, ALU.mult).then_inc(yev, 1)
                    if e:
                        dve.wait_ge(yev, reads)
                        v.tensor_tensor(acc[par][:], acc[par][:], z[:], ALU.add).then_inc(zfin if e == E - 1 else yadd, 1)

                def update(i, tp, par):
                    dve.wait_ge(yT_ps, i + 1)
                    for b in range(NB):
                        ub = u[:, ds(tp * TILE + b * P, P)]
                        last = v.scalar_tensor_tensor(ub, ub, csum[par][:, b:b + 1], ps_t[:, b * P:(b + 1) * P], ALU.mult, ALU.add)
                    last.then_inc(upd, 1)

                def prep_stats(t, n):
                    for b in range(NB):
                        last = v.bn_stats(bn[:, b, :], u[:, ds(t * TILE + b * P, P)])
                    last.then_inc(p_bn, 1)

                def prep_aggr(n):
                    dve.wait_ge(p_bn, n + 1).then_inc(s_alone, 1)
                    for b in range(NB):
                        last = v.bn_aggr(mv[:, b, :], bn[:, b, :])
                    last.then_inc(p_mv, 1)

                def prep_norm(t, n):
                    dve.wait_ge(p_rs, n + 1)
                    for b in range(NB):
                        last = v.tensor_scalar(xh[:, b * P:(b + 1) * P], u[:, ds(t * TILE + b * P, P)], mv[:, b, 0:1],
                                               rs[:, b:b + 1], ALU.subtract, ALU.mult)
                    last.then_inc(p_xh, 1)

                def prep_rest(n, par):
                    dve.wait_ge(p_xhi, n + 1)
                    v.tensor_tensor(xTl[par][:], ps_t[:], xTh[par][:].bitcast(F32), ALU.subtract).then_inc(p_xlo, 1)

                def over_blocks(ap):
                    return ap.unsqueeze(1).to_broadcast([P, NB, E])

                def over_experts(ap):
                    return ap.unsqueeze(2).to_broadcast([P, NB, E])

                def link(n, k):
                    dve.wait_ge(p_link, n * LINKS + k)

                def router_logits(l, n):
                    dve.wait_ge(p_lg_ps, n + 1)
                    dve.wait_ge(p_sd, n + 1)
                    v.reduce_sum(lg[:], ps_r[:, LG].rearrange("p (b h e) -> p b e h", b=NB, h=2), axis=AX.X).then_inc(p_link, 1)
                    v.tensor_tensor(t2[:], mv[:, :, 0:1].to_broadcast([P, NB, E]), over_blocks(cs[:, ds(l * E, E)]), ALU.mult)
                    link(n, 1)
                    v.tensor_tensor(t1[:], lg[:], over_experts(sd[:]), ALU.mult).then_inc(p_link, 1)
                    link(n, 2)
                    v.tensor_tensor(t3[:], t1[:], t2[:], ALU.add).then_inc(p_link, 1)
                    link(n, 3)
                    v.tensor_tensor(lgf[:], t3[:], over_blocks(rb[:, ds(l * E, E)]), ALU.add).then_inc(p_link, 1)

                def router_rank(n):
                    link(n, 4)
                    v.tensor_tensor(dd[:], lgf[:].unsqueeze(2).to_broadcast([P, NB, E, E]),
                                    lgf[:].unsqueeze(3).to_broadcast([P, NB, E, E]), ALU.subtract).then_inc(p_link, 1)
                    link(n, 5)
                    v.tensor_tensor(cc[:].rearrange("p b e f -> p b (e f)"), dd[:].rearrange("p b e f -> p b (e f)"),
                                    order[:].unsqueeze(1).to_broadcast([P, NB, E * E]), ALU.is_ge).then_inc(p_link, 1)
                    link(n, 6)
                    v.reduce_sum(rank[:], cc[:], axis=AX.X).then_inc(p_link, 1)
                    link(n, 7)
                    v.tensor_scalar(first[:], rank[:], 0.0, None, ALU.is_equal)
                    v.tensor_scalar(top2[:], rank[:], 2.0, 0.5, ALU.is_lt, ALU.mult).then_inc(p_link, 1)

                def router_difference(n):
                    link(n, 8)
                    v.scalar_tensor_tensor(second_first[:], rank[:], 1.0, first[:], ALU.is_equal, ALU.subtract).then_inc(p_link, 1)
                    link(n, 9)
                    v.tensor_tensor(signed[:], second_first[:], lgf[:], ALU.mult).then_inc(p_link, 1)
                    link(n, 10)
                    v.reduce_sum(ndiff[:], signed[:], axis=AX.X).then_inc(p_nd, 1)

                def router_shares(n, par):
                    dve.wait_ge(p_th, n + 1)
                    v.scalar_tensor_tensor(shift[:], second_first[:], -0.5, over_experts(th[:]), ALU.mult, ALU.mult).then_inc(p_link, 1)
                    link(n, 11)
                    v.tensor_tensor(comb[:].rearrange("p e b -> p b e"), shift[:], top2[:], ALU.add).then_inc(p_comb, 1)
                    dve.wait_ge(p_comb, n + 1)
                    v.reduce_sum(csum[par][:], comb[:].rearrange("p e b -> p b e"), axis=AX.X).then_inc(p_sum, 1)

                def rest_w1(l, e, n):
                    dve.wait_ge(c1h, n)
                    v.scalar_tensor_tensor(w1l[:, e * F:(e + 1) * F], w1s[:, e * F:(e + 1) * F], cols[:, ds(l * E + e + LNG, 1)],
                                           w1h[:, e * F:(e + 1) * F].bitcast(F32), ALU.mult, ALU.subtract).then_inc(c1, 1)

                def rest_w2(e, n):
                    dve.wait_ge(c2h, n)
                    v.tensor_tensor(w2l[:, e * F:(e + 1) * F], w2s[:, e * F:(e + 1) * F],
                                    w2h[:, e * F:(e + 1) * F].bitcast(F32), ALU.subtract).then_inc(c2, 1)

                def finish_stats(t, i):
                    dve.wait_ge(upd, i + 1).then_inc(s_alone, 1)
                    for b in range(NB):
                        last = v.bn_stats(fbn[:, b, :], u[:, ds(t * TILE + b * P, P)])
                    last.then_inc(f_bn, 1)
                    dve.wait_ge(f_bn, t + 1).then_inc(s_alone, 1)
                    for b in range(NB):
                        last = v.bn_aggr(fmv[:, b, :], fbn[:, b, :])
                    last.then_inc(f_mv, 1)

                def finish_sum(t, par):
                    dve.wait_ge(f_rs, t + 1)
                    for b in range(NB):
                        last = v.tensor_scalar(fn[:, b * P:(b + 1) * P], u[:, ds(t * TILE + b * P, P)], fmv[:, b, 0:1],
                                               frs[:, b:b + 1], ALU.subtract, ALU.mult)
                    last.then_inc(f_n, 1)
                    dve.wait_ge(f_n, t + 1)
                    dve.wait_ge(f_out[par], t // 2 * 16 + 16)
                    v.tensor_tensor(fo[par][:], fn[:], x1[:, ds(t * TILE, TILE)], ALU.add).then_inc(f_o, 1)

                def combine_before(i, e, par):
                    bcol = (i + NT - 1) // NT * E + B2 - E
                    combine(None, e, par, bcol, i * (K // 2) - 6 + 2 * e + PAIRS, i * E + e - 1, i * 2 + e - 1)

                def step(l, t, par, start=False, end=False, fin=False, nxt=True):
                    i = l * NT + t
                    tp = (i + NT - 1) % NT
                    tn, ln = (0, l + 1) if end else (t + 1, l)
                    for j in range(K // 2):
                        rest(i, j)
                        if j == 0 and nxt:
                            prep_stats(tn, i + 1)
                        if j == 1:
                            if nxt:
                                prep_aggr(i + 1)
                            combine_before(i, 2, 1 - par)
                        if j == 2 and nxt:
                            prep_norm(tn, i + 1)
                        if j == 3:
                            combine_before(i, 3, 1 - par)
                        if j == 4 and nxt:
                            prep_rest(i + 1, 1 - par)
                        if j == 5:
                            combine(i, 0, par, l * E + B2, i * (K // 2) + 2 + PAIRS, None, None)
                            if nxt:
                                router_logits(ln, i + 1)
                        if j == 6:
                            if nxt:
                                router_rank(i + 1)
                                router_difference(i + 1)
                            update(i, tp, 1 - par)
                            if fin:
                                finish_stats(t - 1, i)
                        if j == 7:
                            combine(i, 1, par, l * E + B2, i * (K // 2) + 4 + PAIRS, i * E + 4, i + 1)
                            if nxt:
                                router_shares(i + 1, 1 - par)
                            if fin:
                                finish_sum(t - 1, 1 - par)
                        if end and j % 2 == 1:
                            rest_w1(l + 1, j // 2, l * E + E + j // 2 + 1)
                        if end and j in (5, 7):
                            rest_w2((j - 5) // 2, l * E + E + (j - 5) // 2 + 1)
                        if start and j in (1, 3):
                            rest_w2(j // 2 + 2, l * E + j // 2 + 3)

                dve.sem_inc(lo, PAIRS)
                dve.sem_inc(yadd, 1)
                rwv = rw[:].rearrange("p (l e) -> p l e", l=L)
                rpv = rwp[:].rearrange("p (l h e) -> p l h e", l=L, h=2)
                v.tensor_copy(rpv[:, :, 0, :], rwv).then_inc(s_whi, 1)
                dve.wait_ge(s_whi, 1)
                v.tensor_tensor(rpv[:, :, 1, :], rwv, rpv[:, :, 0, :].bitcast(F32), ALU.subtract).then_inc(s_rwp, 1)
                prep_stats(0, 0)
                prep_aggr(0)
                v.memset(acc[1][:], 0.0)
                v.memset(cb[1][:, 2:4, :], 0.0)
                v.memset(csum[1][:], 1.0)
                v.memset(ps_y[0][:], 0.0)
                v.memset(ps_y[1][:], 0.0).then_inc(s_zero, 1)
                for e in range(E):
                    rest_w1(0, e, e + 1)
                prep_norm(0, 0)
                prep_rest(0, 0)
                rest_w2(0, 1)
                rest_w2(1, 2)
                router_logits(0, 0)
                router_rank(0)
                router_difference(0)
                router_shares(0, 0)
                dve.wait_ge(s_zero, 1)
                steps(dve, step)
                i = L * NT
                combine_before(i, 2, 1)
                combine_before(i, 3, 1)
                update(i, NT - 1, 1)
                finish_stats(NT - 1, i)
                finish_sum(NT - 1, 1)

            @block.tensor
            def _(pe):
                mm = nc.tensor.matmul

                def blk(b):
                    return slice(b * P, (b + 1) * P)

                def first(i, k, par):
                    n = k % BANKS
                    if k == 0:
                        pe.wait_ge(p_xlo, i + 1)
                    pe.wait_ge(gel, i * K + k + 1)
                    c = slice(k * P, (k + 1) * P)
                    mm(ps_h[n][:], w1h[:, c], xTh[par][:], start=True, stop=False)
                    mm(ps_h[n][:], w1h[:, c], xTl[par][:], start=False, stop=False)
                    mm(ps_h[n][:], w1l[:, c], xTh[par][:], start=False, stop=True).then_inc(s1, 1)

                def second(i, k):
                    e = k // FC
                    if k % FC == 0:
                        pe.wait_ge(yev, i * E + e + 1)
                    if k % 2 == 0:
                        pe.wait_ge(lo, i * (K // 2) + k // 2 + 1 + PAIRS)
                    c = slice(k * P, (k + 1) * P)
                    h = slice(k % 2 * TILE, (k % 2 + 1) * TILE)
                    y, n = ps_y[e % 2], k // 2 % PAIRS
                    mm(y[:], w2h[:, c], hh[n][:, h], start=k % FC == 0, stop=False)
                    mm(y[:], w2h[:, c], hl[n][:, h], start=False, stop=False)
                    last = mm(y[:], w2l[:, c], hh[n][:, h], start=False, stop=k % FC == FC - 1)
                    if k % 2:
                        last.then_inc(s2, 1)

                def y_tokens(i, par):
                    pe.wait_ge(zfin, i + 1)
                    for b in range(NB):
                        last = nc.tensor.transpose(ps_t[:, blk(b)], acc[par][:, blk(b)], ident[:])
                    last.then_inc(yT_ps, 1)

                def prep_x(n):
                    pe.wait_ge(p_xh, n + 1)
                    for b in range(NB):
                        last = nc.tensor.transpose(ps_t[:, blk(b)], xh[:, blk(b)], ident[:])
                    last.then_inc(p_xT_ps, 1)

                def prep_logits(l, n, par):
                    pe.wait_ge(p_xlo, n + 1)
                    if not isinstance(n, int) or n > 0:
                        pe.wait_ge(p_cT, n)
                    w = rwp[:, ds(l * 2 * E, 2 * E)]
                    for b in range(NB):
                        o = ps_r[:, b * 2 * E:(b + 1) * 2 * E]
                        mm(o, xTh[par][:, blk(b)], w, start=True, stop=False)
                        last = mm(o, xTl[par][:, blk(b)], w, start=False, stop=True)
                    last.then_inc(p_lg_ps, 1)

                def prep_combT(n):
                    pe.wait_ge(p_comb, n + 1)
                    nc.tensor.transpose(ps_r[0:E * NB, CT], comb[:].rearrange("p e b -> p (e b)"), ident[:]).then_inc(p_cT_ps, 1)

                def step(l, t, par, start=False, end=False, fin=False, nxt=True):
                    i = l * NT + t
                    ln = l + 1 if end else l
                    for k in range(K):
                        if k == 0:
                            pe.wait_ge(c1, l * E + E)
                            pe.wait_ge(c2, l * E + 2)
                        if start and k in (2 * FC, 3 * FC):
                            pe.wait_ge(c2, l * E + k // FC + 1)
                        if k < K - LEAD:
                            first(i, k + LEAD, par)
                        elif nxt:
                            k1 = k + LEAD - K
                            if end and k1 % FC == 0:
                                pe.wait_ge(c1, l * E + E + k1 // FC + 1)
                            first(i + 1, k1, 1 - par)
                        second(i, k)
                        if k == 1 and nxt:
                            pe.wait_ge(upd, i)
                            prep_x(i + 1)
                        if k == 4 and nxt:
                            prep_logits(ln, i + 1, 1 - par)
                        if k == 6:
                            y_tokens(i, 1 - par)
                        if k == 10 and nxt:
                            prep_combT(i + 1)

                pe.sem_inc(s2, PAIRS)
                prep_x(0)
                pe.wait_ge(s_rwp, 1)
                prep_logits(0, 0, 0)
                prep_combT(0)
                pe.wait_ge(c1, E)
                for k in range(LEAD):
                    first(0, k, 0)
                steps(pe, step)
                y_tokens(L * NT, 1)


_INS = ['L0_attn_x', 'L0_attn_wqkv', 'L0_attn_wo', 'L0_ffn_router_w', 'L0_ffn_router_b', 'L0_ffn_ln_g', 'L0_ffn_ln_b',
        'L0_ffn_w1', 'L0_ffn_b1', 'L0_ffn_w2', 'L0_ffn_b2']
_OUT = (BATCH, SEQ, D)


def kernel(**inputs):
    import numpy as _np
    import concourse.bacc as _bacc
    from concourse import mybir as _mybir
    from concourse.bass_utils import run_bass_kernel_spmd as _run

    nc = _bacc.Bacc("TRN2", target_bir_lowering=False, num_devices=1)
    arrays, args = {}, []
    for name in _INS:
        a = _np.ascontiguousarray(inputs[name])
        arrays[f"in_{name}_dram"] = a
        args.append(nc.dram_tensor(f"in_{name}_dram", a.shape, _mybir.dt.from_np(a.dtype), kind="ExternalInput").ap())
    args.append(nc.dram_tensor("out_0_dram", _OUT, F32, kind="ExternalOutput").ap())
    sandwich_kernel(nc, *args)
    r = _run(nc, [arrays], core_ids=[0])
    return r.results[0]["out_0_dram"]
```

```python
import concourse.bass as bass
from concourse import mybir
from contextlib import ExitStack

F32 = mybir.dt.float32
F32R = mybir.dt.float32r
ALU = mybir.AluOpType
ACT = mybir.ActivationFunctionType
AX = mybir.AxisListType
ds = bass.ds

P = 128
BATCH, SEQ, D = 32, 256, 128
TOKENS = BATCH * SEQ
TILE = 512
NT = TOKENS // TILE
NB = TILE // P
HEADS, HD = 16, 8
G = 4
J = HEADS // G
R = 2
JR = HEADS // R
C = 64
PRIOR = SEQ // C - 1
L, E, F, FC = 4, 4, 512, 4
K = E * FC
EPS = 1e-5
TINY, NEVER = 1.2e-38, 3.0e38
BANKS = 4
PAIRS = 4
LEAD = 2 * PAIRS


def sandwich_kernel(nc, x, wqkv, wo, router_w, router_b, ln_g, ln_b, w1, b1, w2, b2, out):
    ctx = ExitStack()
    with ctx:
        def sb(name, shape, dt=F32, to=ctx):
            return to.enter_context(nc.sbuf_tensor(name, shape, dt))

        def sem(name):
            return ctx.enter_context(nc.semaphore(name))

        x1 = sb("x1", [P, NT * TILE])
        u = sb("u", [P, NT * TILE])
        w1s = sb("w1s", [P, E * F])
        w2s = sb("w2s", [P, E * FC * D])
        ident = sb("ident", [P, P])
        rows = sb("rows", [112, P])
        cols = sb("cols", [P, 112])
        b1f = sb("b1f", [P, L * K])
        rw = sb("rw", [P, L * E])
        rwp = sb("rwp", [P, L * 2 * E], F32R)
        cs = sb("cs", [P, L * E])
        rb = sb("rb", [P, L * E])
        onesf = sb("onesf", [P, P])
        order = sb("order", [P, E * E])
        half = sb("half", [P, NB])
        epsc = sb("epsc", [P, NB])
        LNG, LNB, B2 = 64, 80, 96

        s_wqkv, s_small, s_w1, s_w2 = sem("wqkv_in"), sem("small_in"), sem("w1_in"), sem("w2_in")
        s_pool0, s_pool1, s_pool2 = sem("pool_memset"), sem("pool_select"), sem("pool_bd")
        s_const = sem("constants_done")
        s_cols_ps, s_cols = sem("cols_psum"), sem("cols_ready")
        s_b1rows_ps, s_b1rows, s_b1_ps = sem("b1_rows_psum"), sem("b1_rows"), sem("b1_psum")
        s_whi, s_w1all = sem("router_high"), sem("w1_all_in")
        s_rwp = sem("router_split")
        s_alone = sem("wait_alone")
        s_x = sem("x_in")
        a_bn, a_mv, a_rs, a_ve, a_xn = sem("a_bn"), sem("a_mv"), sem("a_rstd"), sem("a_ve"), sem("a_xn")
        a_xT_ps, a_xT = sem("a_xT_psum"), sem("a_xT")
        a_q_ps, a_q, a_qx = sem("a_q_psum"), sem("a_q"), sem("a_q_spread")
        a_k_ps, a_k = sem("a_k_psum"), sem("a_k")
        a_kvtok_ps, a_kv = sem("a_kv_tokens_psum"), sem("a_kv_tokens")
        a_state_ps, a_state = sem("a_state_psum"), sem("a_state")
        a_cum, a_qc, a_den_ps, a_den, a_rec = sem("a_cumk"), sem("a_qcumk"), sem("a_den_psum"), sem("a_den"), sem("a_rec")
        a_s_ps, a_s = sem("a_scores_psum"), sem("a_scores")
        a_num = sem("a_num_psum")
        a_y = sem("a_y")
        a_o_ps, a_o, a_on = sem("a_o_psum"), sem("a_o"), sem("a_o_normed")
        a_x1 = sem("a_x1")
        a_u = sem("a_u")

        x_t = x.rearrange("(t s) n d -> t (s n) d", t=NT)
        x_t = x_t.rearrange("t (b p) d -> t p b d", p=P)
        out_t = out.rearrange("(t s) n d -> t (s n) d", t=NT).rearrange("t (b p) d -> t p b d", p=P)

        def blocks(ap):
            return ap.rearrange("p (b n) -> p b n", b=NB)

        att = ExitStack()
        with att:
            def asb(name, shape, dt=F32):
                return sb(name, shape, dt, att)

            def aps(name):
                return att.enter_context(nc.psum_tensor(name, [P, 512], F32))

            wqkv_sb, wo_sb = asb("wqkv_sb", [P, 3 * D]), asb("wo_sb", [P, D])
            causal128 = asb("causal128", [P, P])
            causal = asb("causal", [P, C])
            headbd = asb("headbd", [P, P])
            jmask = asb("jmask", [P, JR])
            ones = asb("ones", [P, SEQ])
            bn = asb("bn", [P, NB, 6])
            mv = asb("mv", [P, NB, 2])
            ve, rs = asb("ve", [P, NB]), asb("rs", [P, NB])
            xn = asb("xn", [P, TILE])
            xnT = asb("xnT", [P, TILE])
            qT = [asb(f"qT{i}", [P, TILE]) for i in range(2)]
            kT = [asb(f"kT{i}", [P, TILE]) for i in range(2)]
            qx = [asb(f"qx{i}", [P, JR, TILE]) for i in range(2)]
            VX = J * (D + HD)
            vx = [asb(f"vx{i}", [P, NB, VX]) for i in range(2)]
            ktok = asb("ktok", [P, 2, 2, D])
            state = [asb(f"state{i}", [P, 2, PRIOR, D]) for i in range(2)]
            cumk, qcumk = asb("cumk", [P, TILE]), asb("qcumk", [P, TILE])
            sc = [asb(f"sc{i}", [P, HEADS * C]) for i in range(2)]
            w1all = asb("w1all", [P, (L - 1) * E * F])
            den, yT = asb("den", [P, TILE]), asb("yT", [P, TILE])
            rec = asb("rec", [P, TILE])
            o_sb, on = asb("o_sb", [P, TILE]), asb("on", [P, TILE])
            ps_s = [[aps(f"ps_s{n}{r}") for r in range(R)] for n in range(2)]
            ps_num = [aps(f"ps_num{c}") for c in range(2)]
            ps_a, ps_b = aps("ps_a"), aps("ps_b")
            by_seq = (ps_b, ps_a)
            ps_b1 = ps_s[0] + ps_s[1]
            b1_rows = qx[0]

            def own_heads(buf, b):
                v = buf[:, b, :].rearrange("p (j n) -> p j n", j=J)[:, :, 0:D]
                return v.rearrange("p j (g x) -> p j g x", g=G)[:, :, :, 0:HD]

            block = att.enter_context(nc.Block())

            @block.sync
            def _(sp):
                sp.dma_start(blocks(x1[:, 0:TILE]), x_t[0]).then_inc(s_x, 16)
                sp.dma_start(wqkv_sb[:], wqkv).then_inc(s_wqkv, 16)
                sp.dma_start(wo_sb[:], wo).then_inc(s_wqkv, 16)
                with sp.Fori(1, NT) as t:
                    sp.wait_ge(s_x, t * 16)
                    sp.dma_start(blocks(x1[:, ds(t * TILE, TILE)]), x_t[ds(t, 1)].rearrange("o p b d -> p (o b) d")).then_inc(s_x, 16)
                sp.dma_start(rows[0:64, :], b1.rearrange("l e (c p) -> (l e c) p", p=P)).then_inc(s_small, 16)
                sp.dma_start(rows[LNG:LNG + 16, :], ln_g.rearrange("l e h -> (l e) h")).then_inc(s_small, 16)
                sp.dma_start(rows[LNB:LNB + 16, :], ln_b.rearrange("l e h -> (l e) h")).then_inc(s_small, 16)
                sp.dma_start(rows[B2:B2 + 16, :], b2.rearrange("l e h -> (l e) h")).then_inc(s_small, 16)
                sp.dma_start(rw[:].rearrange("h (l e) -> h l e", l=L), router_w.rearrange("l h e -> h l e")).then_inc(s_small, 16)
                sp.dma_start(rb[:], router_b.rearrange("l e -> (l e)").partition_broadcast(P)).then_inc(s_small, 16)
                for l in range(1, L):
                    sp.dma_start(w1all[:, (l - 1) * E * F:l * E * F].rearrange("h (e f) -> h e f", e=E),
                                 w1[l].rearrange("e h f -> h e f")).then_inc(s_w1all, 16)
                sp.dma_start(w1s[:].rearrange("h (e f) -> h e f", e=E), w1[0].rearrange("e h f -> h e f")).then_inc(s_w1, 16)
                for e in range(E):
                    sp.dma_start(blocks(w2s[:, e * F:(e + 1) * F]),
                                 w2[0, e].rearrange("(c p) h -> p c h", p=P)).then_inc(s_w2, 16)

            @block.gpsimd
            def _(pool):
                g = nc.gpsimd
                g.memset(ident[:], 0.0)
                g.memset(causal128[:], 1.0)
                g.memset(headbd[:], 1.0)
                g.memset(ones[:], 1.0)
                g.memset(half[:], -0.5)
                g.memset(epsc[:], EPS)
                g.memset(onesf[:], 1.0)
                g.memset(order[:], 0.0).then_inc(s_pool0, 1)
                pool.wait_ge(s_pool0, 1)
                g.affine_select(out=ident[:], in_=ident[:], compare_op=ALU.not_equal, fill=1.0, base=0,
                                pattern=[[-1, P]], channel_multiplier=1)
                g.affine_select(out=causal128[:], in_=causal128[:], compare_op=ALU.is_ge, fill=0.0, base=0,
                                pattern=[[1, P]], channel_multiplier=-1)
                g.affine_select(out=headbd[:], in_=headbd[:], compare_op=ALU.is_ge, fill=0.0, base=0,
                                pattern=[[-HD, HEADS], [0, HD]], channel_multiplier=1).then_inc(s_pool1, 1)
                for e in range(E):
                    g.memset(order[:, e * E + e:e * E + e + 1], NEVER)
                    if e < E - 1:
                        g.memset(order[:, e * E + e + 1:(e + 1) * E], TINY)
                pool.wait_ge(s_pool1, 1)
                g.affine_select(out=headbd[:], in_=headbd[:], compare_op=ALU.is_ge, fill=0.0, base=HD - 1,
                                pattern=[[HD, HEADS], [0, HD]], channel_multiplier=-1).then_inc(s_const, 1)

                def rstd(n):
                    pool.wait_ge(a_mv, n + 1)
                    g.tensor_tensor(ve[:], mv[:, :, 1], epsc[:], ALU.add).then_inc(a_ve, 1)
                    pool.wait_ge(a_ve, n + 1)
                    g.tensor_tensor(rs[:], ve[:], half[:], ALU.pow).then_inc(a_rs, 1)

                with pool.Fori(0, 3 * NT) as n:
                    rstd(n)

            def normed(dst, src, b):
                return nc.vector.tensor_scalar(dst, src, mv[:, b, 0:1], rs[:, b:b + 1], ALU.subtract, ALU.mult)

            @block.vector
            def _(dve):
                v = nc.vector

                def stats(src, n):
                    for b in range(NB):
                        last = v.bn_stats(bn[:, b, :], src(b))
                    last.then_inc(a_bn, 1)
                    dve.wait_ge(a_bn, n + 1).then_inc(s_alone, 1)
                    for b in range(NB):
                        last = v.bn_aggr(mv[:, b, :], bn[:, b, :])
                    last.then_inc(a_mv, 1)

                def x_stats(t, n):
                    dve.wait_ge(s_x, t * 16 + 16).then_inc(s_alone, 1)
                    stats(lambda b: x1[:, ds(t * TILE + b * P, P)], n)

                def x_norm(t, n):
                    dve.wait_ge(a_rs, n + 1)
                    for b in range(NB):
                        last = normed(xn[:, b * P:(b + 1) * P], x1[:, ds(t * TILE + b * P, P)], b)
                    last.then_inc(a_xn, 1)

                def make_state(t, par, s):
                    dve.wait_ge(a_state_ps, t * 2 + s + 1)
                    v.tensor_tensor(state[par][:, s], by_seq[s][:, 0:PRIOR * D].rearrange("p (k n) -> p k n", k=PRIOR),
                                    headbd[:].unsqueeze(1).to_broadcast([P, PRIOR, P]), ALU.mult).then_inc(a_state, 1)

                def q_cumk(t, par):
                    dve.wait_ge(a_k, t + 1)
                    for s in range(2):
                        c = slice(s * SEQ, (s + 1) * SEQ)
                        last = v.tensor_tensor_scan(cumk[:, c], ones[:], kT[par][:, c], 0.0, ALU.mult, ALU.add)
                    last.then_inc(a_cum, 1)
                    dve.wait_ge(a_cum, t + 1)
                    v.tensor_tensor(qcumk[:], qT[par][:], cumk[:], ALU.mult).then_inc(a_qc, 1)

                def reciprocal(t, part):
                    if part == 0:
                        dve.wait_ge(a_den, t + 1)
                        if not isinstance(t, int) or t > 0:
                            dve.wait_ge(a_y, t)
                    c = slice(part * P, (part + 1) * P)
                    last = v.reciprocal(rec[:, c], den[:, c])
                    if part == NB - 1:
                        last.then_inc(a_rec, 1)

                def mask(t, b, fresh):
                    if not fresh:
                        dve.wait_ge(a_num, t * NB + b - 1)
                    for r in range(R):
                        dve.wait_ge(a_s_ps, t * 8 + b * R + r + 1)
                        v.tensor_tensor(sc[b % 2][:, r * JR * C:(r + 1) * JR * C].rearrange("p (j n) -> p j n", j=JR),
                                        ps_s[b % 2][r][:].rearrange("p (j n) -> p j n", j=JR),
                                        causal[:].unsqueeze(1).to_broadcast([P, JR, C]), ALU.mult).then_inc(a_s, 1)

                def divide(t):
                    dve.wait_ge(a_num, t * NB + NB)
                    dve.wait_ge(a_rec, t + 1)
                    for c in range(2):
                        def chunks(ap):
                            return ap.rearrange("p (b c n) -> p b c n", b=NB, c=2)[:, :, c, :]
                        last = v.tensor_tensor(chunks(yT[:]), ps_num[c][:, 0:NB * C].rearrange("p (b n) -> p b n", b=NB),
                                               chunks(rec[:]), ALU.mult)
                    last.then_inc(a_y, 1)

                def o_stats(t, n):
                    dve.wait_ge(a_o, t + 1).then_inc(s_alone, 1)
                    stats(lambda b: o_sb[:, b * P:(b + 1) * P], n)

                def make_x1(t, n):
                    dve.wait_ge(a_rs, n + 1)
                    for b in range(NB):
                        last = normed(on[:, b * P:(b + 1) * P], o_sb[:, b * P:(b + 1) * P], b)
                    last.then_inc(a_on, 1)
                    dve.wait_ge(a_on, t + 1)
                    xt = x1[:, ds(t * TILE, TILE)]
                    v.tensor_tensor(xt, xt, on[:], ALU.add).then_inc(a_x1, 1)

                def x1_stats(t, n):
                    dve.wait_ge(a_x1, t + 1).then_inc(s_alone, 1)
                    stats(lambda b: x1[:, ds(t * TILE + b * P, P)], n)

                def make_u(t, n):
                    dve.wait_ge(a_rs, n + 1)
                    for b in range(NB):
                        last = normed(u[:, ds(t * TILE + b * P, P)], x1[:, ds(t * TILE + b * P, P)], b)
                    last.then_inc(a_u, 1)

                def body(t, par, prev, nxt, n):
                    m = n + 1 if nxt else n
                    if prev:
                        divide(t - 1)
                    if nxt:
                        x_stats(t + 1, n)
                    mask(t, 0, not prev)
                    if nxt:
                        x_norm(t + 1, n)
                    mask(t, 1, not prev)
                    reciprocal(t, 0)
                    if prev:
                        o_stats(t - 1, m)
                    mask(t, 2, False)
                    reciprocal(t, 1)
                    if prev:
                        make_x1(t - 1, m)
                        x1_stats(t - 1, m + 1)
                    mask(t, 3, False)
                    if nxt:
                        q_cumk(t + 1, 1 - par)
                    reciprocal(t, 2)
                    if nxt:
                        make_state(t + 1, 1 - par, 0)
                        make_state(t + 1, 1 - par, 1)
                    if prev:
                        make_u(t - 1, m + 1)
                    reciprocal(t, 3)

                x_stats(0, 0)
                x_norm(0, 0)
                for par in range(2):
                    v.memset(vx[par][:], 0.0)
                dve.wait_ge(s_const, 1)
                for c in range(2):
                    v.tensor_copy(causal[c * C:(c + 1) * C, :], causal128[c * C:(c + 1) * C, c * C:(c + 1) * C])
                v.reduce_sum(jmask[:], headbd[:].rearrange("p (r j e) -> p j r e", r=R, j=JR)[:, :, :, 0], axis=AX.X).then_inc(s_pool2, 1)
                q_cumk(0, 0)
                make_state(0, 0, 0)
                make_state(0, 0, 1)
                body(0, 0, False, True, 1)
                body(1, 1, True, True, 2)
                with dve.Fori(1, NT // 2 - 1) as q:
                    body(q * 2, 0, True, True, q * 6 - 1)
                    body(q * 2 + 1, 1, True, True, q * 6 + 2)
                body(NT - 2, 0, True, True, 3 * NT - 7)
                body(NT - 1, 1, True, False, 3 * NT - 4)
                divide(NT - 1)
                o_stats(NT - 1, 3 * NT - 2)
                make_x1(NT - 1, 3 * NT - 2)
                x1_stats(NT - 1, 3 * NT - 1)
                make_u(NT - 1, 3 * NT - 1)
                for l in range(L):
                    dve.wait_ge(s_b1_ps, l + 1)
                    c = slice(l * K, (l + 1) * K)
                    v.tensor_tensor(b1f[:, c].rearrange("p (e c) -> p c e", e=E),
                                    ps_b1[l][:].rearrange("p (c e x) -> p c e x", c=FC, e=E)[:, :, :, 0],
                                    cols[:, c].rearrange("p (e c) -> p c e", e=E), ALU.add)

            @block.scalar
            def _(act):
                a = nc.scalar

                def copy_o(t):
                    act.wait_ge(a_o_ps, t + 1)
                    if not isinstance(t, int) or t > 0:
                        act.wait_ge(a_on, t)
                    a.activation(o_sb[:], ps_b[:], ACT.Identity).then_inc(a_o, 1)

                def spread_q(par, heads):
                    for j in heads:
                        last = a.activation(qx[par][:, j, :], qT[par][:], ACT.Identity, scale=jmask[:, j:j + 1])
                    return last

                def evacuate(t, par):
                    act.wait_ge(a_xT_ps, t + 1)
                    a.activation(xnT[:], ps_a[:], ACT.Identity).then_inc(a_xT, 1)
                    act.wait_ge(a_q_ps, t + 1)
                    a.activation(qT[par][:], ps_b[:], ACT.Relu).then_inc(a_q, 1)
                    act.wait_ge(a_k_ps, t + 1)
                    a.activation(kT[par][:], ps_a[:], ACT.Relu).then_inc(a_k, 1)
                    act.wait_ge(a_q, t + 1)
                    if isinstance(t, int) and t == 0:
                        act.wait_ge(s_pool2, 1)
                    spread_q(par, range(3))
                    for s in range(2):
                        act.wait_ge(a_kvtok_ps, t * 2 + s + 1)
                        a.activation(ktok[:, s], by_seq[s][:].rearrange("p (b w n) -> p b w n", b=2, w=2)[:, :, 0, :],
                                     ACT.Relu)
                        for b in range(2):
                            last = a.activation(own_heads(vx[par], 2 * s + b), by_seq[s][:, b * 2 * D + D:(b + 1) * 2 * D].rearrange(
                                "p (g j e) -> p j g e", g=G, j=J), ACT.Identity)
                        last.then_inc(a_kv, 1)
                    spread_q(par, range(3, JR)).then_inc(a_qx, 1)
                    act.wait_ge(a_den_ps, t + 1)
                    if not isinstance(t, int) or t > 0:
                        act.wait_ge(a_rec, t)
                    a.activation(den[:], ps_a[:], ACT.Identity, bias=epsc[:, 0:1]).then_inc(a_den, 1)

                evacuate(0, 0)
                evacuate(1, 1)
                copy_o(0)
                evacuate(2, 0)
                copy_o(1)
                evacuate(3, 1)
                with act.Fori(2, NT // 2) as q:
                    copy_o(q * 2 - 2)
                    evacuate(q * 2, 0)
                    copy_o(q * 2 - 1)
                    evacuate(q * 2 + 1, 1)
                copy_o(NT - 2)
                act.wait_ge(s_cols_ps, 1)
                a.activation(cols[:], ps_a[:, 0:112], ACT.Identity).then_inc(s_cols, 1)
                a.activation(cs[:], ps_a[:, P:P + L * E], ACT.Identity)
                copy_o(NT - 1)
                for l in range(L):
                    act.wait_ge(s_b1rows_ps, l + 1)
                    a.activation(b1_rows[:, l, :], ps_b1[l][:], ACT.Identity).then_inc(s_b1rows, 1)

            @block.tensor
            def _(pe):
                mm = nc.tensor.matmul

                def blk(b):
                    return slice(b * P, (b + 1) * P)

                def transposes(t):
                    pe.wait_ge(a_xn, t + 1)
                    if not isinstance(t, int) or t > 0:
                        pe.wait_ge(a_den, t)
                    for b in range(NB):
                        last = nc.tensor.transpose(ps_a[:, blk(b)], xn[:, blk(b)], ident[:])
                    last.then_inc(a_xT_ps, 1)

                def qk(t):
                    if not isinstance(t, int) or t > 1:
                        pe.wait_ge(a_o, t - 1)
                    pe.wait_ge(a_xT, t + 1)
                    mm(ps_b[:], wqkv_sb[:, 0:D], xnT[:], start=True, stop=True).then_inc(a_q_ps, 1)
                    mm(ps_a[:], wqkv_sb[:, D:2 * D], xnT[:], start=True, stop=True).then_inc(a_k_ps, 1)

                def kv_tokens(t):
                    for s in range(2):
                        pe.wait_ge(a_k if s else a_q, t + 1)
                        for b in range(2):
                            last = mm(by_seq[s][:, b * 2 * D:(b + 1) * 2 * D], xnT[:, blk(2 * s + b)], wqkv_sb[:, D:3 * D],
                                      start=True, stop=True)
                        last.then_inc(a_kvtok_ps, 1)

                def states(t, par):
                    for s in range(2):
                        pe.wait_ge(a_kv, t * 2 + s + 1)

                        def product(k, b, rows, **kw):
                            moving = own_heads(vx[par], 2 * s + b).rearrange("p j g e -> p g j e")[0:rows]
                            out = by_seq[s][:, k * D:(k + 1) * D].rearrange("p (g j e) -> p g j e", g=G, j=J)
                            return mm(out, ktok[0:rows, s, b, :], moving, **kw)

                        product(0, 0, C, start=True, stop=True)
                        product(1, 0, P, start=True, stop=True)
                        product(2, 0, P, start=True, stop=False)
                        product(2, 1, C, start=False, stop=True).then_inc(a_state_ps, 1)

                def denominator(t):
                    pe.wait_ge(a_qc, t + 1)
                    pe.wait_ge(a_state, t * 2 + 2)
                    mm(ps_a[:], headbd[:], qcumk[:], start=True, stop=True).then_inc(a_den_ps, 1)

                def scores(t, par, b, fresh):
                    if b == 0:
                        pe.wait_ge(a_qx, t + 1).then_inc(s_alone, 1)
                    for r in range(R):
                        rows_ = slice(64 * r, 64 * r + 64)
                        if not fresh:
                            pe.wait_ge(a_s, t * 8 + b * R + r - 3).then_inc(s_alone, 1)
                        for c in range(2):
                            tok = slice(b * P + c * C, b * P + (c + 1) * C)
                            last = mm(ps_s[b % 2][r][c * C:(c + 1) * C, :].rearrange("p (j n) -> p j n", j=JR),
                                      kT[par][rows_, tok], qx[par][rows_, :, tok], start=True, stop=True)
                        last.then_inc(a_s_ps, 1)

                def numerator(t, par, b, fresh):
                    if b == 0 and not fresh:
                        pe.wait_ge(a_y, t).then_inc(s_alone, 1)
                    out = slice(b * C, (b + 1) * C)
                    prior = [b % 2 * 2 + c - 1 for c in range(2)]
                    for c in range(2):
                        if prior[c] >= 0:
                            pe.wait_ge(a_state, t * 2 + b // 2 + 1)
                            mm(ps_num[c][:, out], state[par][:, b // 2, prior[c], :], qT[par][:, b * P + c * C:b * P + (c + 1) * C],
                               start=True, stop=False, skip_group_check=True)
                    pe.wait_ge(a_s, t * 8 + b * R + R).then_inc(s_alone, 1)
                    for c in range(2):
                        for j in range(J):
                            for g in range(G):
                                h = g * J + j
                                last = mm(ps_num[c][32 * g:32 * g + 32, out],
                                          vx[par][c * C:(c + 1) * C, b, j * D + 32 * g:j * D + 32 * g + 32],
                                          sc[b % 2][c * C:(c + 1) * C, h * C:(h + 1) * C],
                                          start=j == 0 and prior[c] < 0, stop=j == J - 1, skip_group_check=True)
                    last.then_inc(a_num, 1)

                def project(t):
                    pe.wait_ge(a_y, t + 1)
                    for b in range(NB):
                        last = mm(ps_b[:, blk(b)], yT[:, blk(b)], wo_sb[:], start=True, stop=True)
                    last.then_inc(a_o_ps, 1)

                pe.wait_ge(s_const, 1)
                pe.wait_ge(s_wqkv, 32)
                transposes(0)
                qk(0)
                kv_tokens(0)
                states(0, 0)
                denominator(0)

                def body(t, par, prev, nxt):
                    scores(t, par, 0, not prev)
                    scores(t, par, 1, not prev)
                    if prev:
                        project(t - 1)
                    numerator(t, par, 0, not prev)
                    scores(t, par, 2, False)
                    if nxt:
                        transposes(t + 1)
                    numerator(t, par, 1, False)
                    if nxt:
                        qk(t + 1)
                    scores(t, par, 3, False)
                    if nxt:
                        kv_tokens(t + 1)
                    numerator(t, par, 2, False)
                    if nxt:
                        states(t + 1, 1 - par)
                    numerator(t, par, 3, False)
                    if nxt:
                        denominator(t + 1)

                body(0, 0, False, True)
                body(1, 1, True, True)
                with pe.Fori(1, NT // 2 - 1) as q:
                    body(q * 2, 0, True, True)
                    body(q * 2 + 1, 1, True, True)
                body(NT - 2, 0, True, True)
                body(NT - 1, 1, True, False)
                pe.wait_ge(s_small, 6 * 16)
                pe.wait_ge(a_den, NT)
                nc.tensor.transpose(ps_a[:, 0:112], rows[:], ident[0:112, 0:112])
                mm(ps_a[:, P:P + L * E], onesf[:], rw[:], start=True, stop=True).then_inc(s_cols_ps, 1)
                project(NT - 1)
                pe.wait_ge(s_cols, 1)
                pe.wait_ge(s_w1, 16)
                for l in range(L):
                    if l == 1:
                        pe.wait_ge(s_w1all, (L - 1) * 16)
                    for e in range(E):
                        n = l * E + e
                        weights, at = (w1s, n * F) if l == 0 else (w1all, (n - E) * F)
                        last = mm(ps_b1[l][32 * e:32 * e + 32, :], cols[:, LNB + n:LNB + n + 1].to_broadcast([P, 32]),
                                  weights[:, at:at + F], start=True, stop=True)
                    last.then_inc(s_b1rows_ps, 1)
                for l in range(L):
                    pe.wait_ge(s_b1rows, l + 1)
                    for c in range(FC):
                        last = nc.tensor.transpose(ps_b1[l][:, blk(c)], b1_rows[:, l, blk(c)], ident[:])
                    last.then_inc(s_b1_ps, 1)

        s1 = sem("hidden_psum")
        gel = sem("gelu_done")
        hi = sem("hidden_high")
        lo = sem("hidden_rest")
        s2 = sem("second_done")
        yev = sem("y_read")
        yadd = sem("y_partly_summed")
        zfin = sem("y_summed")
        yT_ps, upd = sem("y_token_major_psum"), sem("u_updated")
        p_bn, p_mv, p_ve, p_rs, p_sd = (sem(f"p_{n}") for n in ("bn", "mv", "ve", "rstd", "std"))
        p_xh, p_xT_ps, p_xhi, p_xlo = (sem(f"p_{n}") for n in ("xhat", "xT_psum", "xT_high", "xT_rest"))
        p_lg_ps, p_nd, p_th, p_comb, p_sum = (sem(f"p_{n}") for n in ("logits_psum", "difference", "tanh", "comb", "combsum"))
        p_cT_ps, p_cT, p_cw, p_bc = (sem(f"p_{n}") for n in ("combT_psum", "combT", "comb_written", "comb_spread"))
        p_link = sem("p_router_chain")
        LINKS = 11
        c1h, c1, c2h, c2 = sem("w1_high"), sem("w1_split"), sem("w2_high"), sem("w2_split")
        s_bias = sem("layer_bias")
        f_bn, f_mv, f_ve, f_rs, f_n, f_o = (sem(f"f_{n}") for n in ("bn", "mv", "ve", "rstd", "norm", "sum"))
        f_out = [sem(f"f_out{n}") for n in range(2)]
        s_zero = sem("step_before_ready")

        comb_rows = nc.dram_tensor("comb_rows", [2, E * TILE], F32).ap()

        exp = ExitStack()
        with exp:
            def esb(name, shape, dt=F32):
                return sb(name, shape, dt, exp)

            def eps(name):
                return exp.enter_context(nc.psum_tensor(name, [P, 512], F32))

            w1h, w1l = esb("w1h", [P, E * F], F32R), esb("w1l", [P, E * F], F32R)
            w2h, w2l = esb("w2h", [P, E * FC * D], F32R), esb("w2l", [P, E * FC * D], F32R)
            hg = [esb(f"hg{n}", [P, 2 * TILE]) for n in range(PAIRS)]
            hh = [esb(f"hh{n}", [P, 2 * TILE], F32R) for n in range(PAIRS)]
            hl = [esb(f"hl{n}", [P, 2 * TILE], F32R) for n in range(PAIRS)]
            xTh = [esb(f"xTh{n}", [P, TILE], F32R) for n in range(2)]
            xTl = [esb(f"xTl{n}", [P, TILE], F32R) for n in range(2)]
            xh = esb("xh", [P, TILE])
            bn, mv = esb("pbn", [P, NB, 6]), esb("pmv", [P, NB, 2])
            ve, rs, sd = esb("pve", [P, NB]), esb("prs", [P, NB]), esb("psd", [P, NB])
            fbn, fmv = esb("fbn", [P, NB, 6]), esb("fmv", [P, NB, 2])
            fve, frs = esb("fve", [P, NB]), esb("frs", [P, NB])
            fu = [esb(f"fu{n}", [P, TILE]) for n in range(2)]
            fn, fo = esb("fn", [P, TILE]), [esb(f"fo{n}", [P, TILE]) for n in range(2)]
            lg, t1, t2, t3, lgf = (esb(n, [P, NB, E]) for n in ("lg", "t1", "t2", "t3", "lgf"))
            dd, cc = esb("dd", [P, NB, E, E]), esb("cc", [P, NB, E, E])
            rank, first, top2, second_first, signed, shift = (
                esb(n, [P, NB, E]) for n in ("rank", "first", "top2", "second_first", "signed", "shift"))
            ndiff, th = esb("ndiff", [P, NB]), esb("th", [P, NB])
            comb = esb("comb", [P, E, NB])
            csum = [esb(f"csum{n}", [P, NB]) for n in range(2)]
            combT = esb("combT", [E * NB, P])
            cb = [esb(f"cb{n}", [P, E, TILE]) for n in range(2)]
            z, acc = esb("z", [P, TILE]), [esb(f"acc{n}", [P, TILE]) for n in range(2)]
            b1c = esb("b1c", [P, K])
            ps_h = [eps(f"ps_h{n}") for n in range(BANKS)]
            ps_y = [eps(f"ps_y{n}") for n in range(2)]
            ps_t = eps("ps_t")
            ps_r = eps("ps_r")
            LG, CT = slice(0, NB * 2 * E), slice(128, 256)

            block = exp.enter_context(nc.Block())

            def steps(eng, step):
                def middle(l, **kw):
                    with eng.Fori(1, NT // 2 - 1) as q:
                        step(l, q * 2, 0, **kw)
                        step(l, q * 2 + 1, 1, **kw)

                with eng.Fori(0, L - 1) as l:
                    step(l, 0, 0, start=True)
                    step(l, 1, 1)
                    middle(l)
                    step(l, NT - 2, 0)
                    step(l, NT - 1, 1, end=True)
                step(L - 1, 0, 0, start=True)
                step(L - 1, 1, 1, fin=True)
                middle(L - 1, fin=True)
                step(L - 1, NT - 2, 0, fin=True)
                step(L - 1, NT - 1, 1, fin=True, nxt=False)

            @block.sync
            def _(sp):
                def spread(n, par):
                    sp.wait_ge(p_cT, n + 1)
                    sp.dma_start(comb_rows[par].rearrange("(r p) -> r p", p=P), combT[:]).then_inc(p_cw, 16)
                    sp.wait_ge(p_cw, n * 16 + 32)
                    if not isinstance(n, int) or n > 0:
                        sp.wait_ge(zfin, n)
                    sp.dma_start(cb[par][:].rearrange("p e n -> p (e n)"), comb_rows[par].partition_broadcast(P)).then_inc(p_bc, 16)

                def step(l, t, par, start=False, end=False, fin=False, nxt=True):
                    i = l * NT + t
                    if nxt:
                        spread(i + 1, 1 - par)
                    if start and not isinstance(l, int):
                        sp.wait_ge(c1, l * E + E)
                        sp.wait_ge(c2, l * E + E)
                        for e in range(E):
                            sp.dma_start(w1s[:, e * F:(e + 1) * F], w1[ds(l + 1, 1), e].rearrange("o h f -> (o h) f")).then_inc(s_w1, 16)
                            sp.dma_start(blocks(w2s[:, e * F:(e + 1) * F]),
                                         w2[ds(l + 1, 1), e].rearrange("o (c p) h -> p (o c) h", p=P)).then_inc(s_w2, 16)
                    if fin:
                        sp.wait_ge(f_o, t)
                        sp.dma_start(out_t[ds(t - 1, 1)].rearrange("o p b d -> p (o b) d"), blocks(fo[1 - par][:])).then_inc(f_out[1 - par], 16)

                sp.sem_inc(p_cw, 16)
                sp.sem_inc(f_out[0], 16)
                sp.sem_inc(f_out[1], 16)
                sp.wait_ge(s_zero, 2)
                spread(0, 0)
                steps(sp, step)
                sp.wait_ge(f_o, NT)
                sp.dma_start(out_t[NT - 1], blocks(fo[1][:])).then_inc(f_out[1], 16)
                sp.wait_ge(f_out[0], NT // 2 * 16 + 16)
                sp.wait_ge(f_out[1], NT // 2 * 16 + 16)

            @block.gpsimd
            def _(pool):
                g = nc.gpsimd

                def prepare(n):
                    pool.wait_ge(p_mv, n + 1)
                    g.tensor_tensor(ve[:], mv[:, :, 1], epsc[:], ALU.add).then_inc(p_ve, 1)
                    pool.wait_ge(p_ve, n + 1)
                    g.tensor_tensor(rs[:], ve[:], half[:], ALU.pow).then_inc(p_rs, 1)
                    pool.wait_ge(p_rs, n + 1)
                    g.tensor_tensor(sd[:], ve[:], rs[:], ALU.mult).then_inc(p_sd, 1)

                def finish(t, par):
                    pool.wait_ge(f_mv, t + 1)
                    g.tensor_tensor(fve[:], fmv[:, :, 1], epsc[:], ALU.add).then_inc(f_ve, 1)
                    pool.wait_ge(f_ve, t + 1)
                    g.tensor_tensor(frs[:], fve[:], half[:], ALU.pow).then_inc(f_rs, 1)
                    pool.wait_ge(f_rs, t + 1).then_inc(s_alone, 1)
                    for b in range(NB):
                        last = g.tensor_scalar(fn[:, b * P:(b + 1) * P], fu[par][:, b * P:(b + 1) * P], fmv[:, b, 0:1],
                                               frs[:, b:b + 1], ALU.subtract, ALU.mult)
                    last.then_inc(f_n, 1)
                    pool.wait_ge(f_n, t + 1)
                    pool.wait_ge(f_out[par], t // 2 * 16 + 16)
                    g.tensor_tensor(fo[par][:], fn[:], x1[:, ds(t * TILE, TILE)], ALU.add).then_inc(f_o, 1)

                def step(l, t, par, start=False, end=False, fin=False, nxt=True):
                    i = l * NT + t
                    if nxt:
                        prepare(i + 1)
                    if fin:
                        finish(t - 1, 1 - par)

                g.memset(cb[1][:, 2:4, :], 0.0)
                g.memset(csum[1][:], 1.0)
                g.memset(acc[1][:], 0.0).then_inc(s_zero, 1)
                prepare(0)
                steps(pool, step)
                finish(NT - 1, 1)

            @block.scalar
            def _(act):
                a = nc.scalar

                def gelu(i, k):
                    act.wait_ge(s1, i * K + k + 1)
                    if k % 2 == 0:
                        act.wait_ge(lo, i * (K // 2) + k // 2 + 1)
                    a.activation(hg[k // 2 % PAIRS][:, k % 2 * TILE:(k % 2 + 1) * TILE], ps_h[k % BANKS][:], ACT.Gelu,
                                 bias=b1c[:, k:k + 1]).then_inc(gel, 1)

                def high(i, j):
                    act.wait_ge(gel, i * K + 2 * j + 2 + BANKS)
                    act.wait_ge(s2, i * (K // 2) + j + 1)
                    a.activation(hh[j % PAIRS][:], hg[j % PAIRS][:], ACT.Identity).then_inc(hi, 1)

                def prep_x(n, par):
                    act.wait_ge(p_xT_ps, n + 1)
                    a.activation(xTh[par][:], ps_t[:], ACT.Identity).then_inc(p_xhi, 1)

                def prep_tanh(n):
                    act.wait_ge(p_nd, n + 1)
                    a.activation(th[:], ndiff[:], ACT.Tanh, scale=-0.5).then_inc(p_th, 1)

                def prep_combT(n):
                    act.wait_ge(p_cT_ps, n + 1)
                    act.wait_ge(p_cw, n * 16 + 16)
                    a.activation(combT[:], ps_r[0:E * NB, CT], ACT.Identity).then_inc(p_cT, 1)

                def split_w1(l, e):
                    a.activation(w1h[:, e * F:(e + 1) * F], w1s[:, e * F:(e + 1) * F], ACT.Identity,
                                 scale=cols[:, ds(l * E + e + LNG, 1)]).then_inc(c1h, 1)

                def split_w2(e):
                    a.activation(w2h[:, e * F:(e + 1) * F], w2s[:, e * F:(e + 1) * F], ACT.Identity).then_inc(c2h, 1)

                def layer_bias(l):
                    a.activation(b1c[:], b1f[:, ds(l * K, K)], ACT.Identity).then_inc(s_bias, 1)
                    act.wait_ge(s_bias, l + 1)

                def step(l, t, par, start=False, end=False, fin=False, nxt=True):
                    i = l * NT + t
                    for j in range(K // 2):
                        high(i, j)
                        if j < K // 2 - 1:
                            gelu(i, 2 * j + 2)
                            gelu(i, 2 * j + 3)
                        elif nxt:
                            if end:
                                act.wait_ge(gel, i * K + K + BANKS).then_inc(s_alone, 1)
                                layer_bias(l + 1)
                            gelu(i + 1, 0)
                            gelu(i + 1, 1)
                        if nxt and j == 3:
                            prep_x(i + 1, 1 - par)
                        if nxt and j == 6:
                            prep_tanh(i + 1)
                        if j == 1:
                            prep_combT(i)
                        if end and j % 2 == 1:
                            e = j // 2
                            if e == 0:
                                act.wait_ge(s_w1, (l + 1) * (E * 16) + 16)
                            act.wait_ge(s1, i * K + (e + 1) * FC).then_inc(s_alone, 1)
                            split_w1(l + 1, e)
                        if end and j in (5, 7):
                            e = (j - 5) // 2
                            if e == 0:
                                act.wait_ge(s_w2, (l + 2) * (E * 16))
                            act.wait_ge(s2, i * (K // 2) + 2 * e + 2 + PAIRS)
                            split_w2(e)
                        if start and j in (4, 6):
                            e = 2 if j == 4 else 3
                            act.wait_ge(s2, i * (K // 2) + e * 2 - 6 + PAIRS)
                            split_w2(e)

                act.sem_inc(gel, BANKS)
                act.wait_ge(s_w1, 16)
                act.wait_ge(s_w2, E * 16)
                for e in range(E):
                    split_w1(0, e)
                split_w2(0)
                split_w2(1)
                layer_bias(0)
                prep_x(0, 0)
                gelu(0, 0)
                gelu(0, 1)
                prep_tanh(0)
                steps(act, step)

            @block.vector
            def _(dve):
                v = nc.vector

                def rest(i, j):
                    dve.wait_ge(hi, i * (K // 2) + j + 1)
                    n = j % PAIRS
                    v.tensor_tensor(hl[n][:], hg[n][:], hh[n][:].bitcast(F32), ALU.subtract).then_inc(lo, 1)

                def combine(n, e, par, bcol, pairs, reads, adds):
                    dve.wait_ge(s2, pairs)
                    if e:
                        dve.wait_ge(zfin if e == 1 else yadd, adds)
                    if e == 0:
                        dve.wait_ge(p_bc, n * 16 + 16)
                    v.scalar_tensor_tensor(acc[par][:] if e == 0 else z[:], ps_y[e % 2][:], cols[:, ds(bcol + e, 1)],
                                           cb[par][:, e, :], ALU.add, ALU.mult).then_inc(yev, 1)
                    if e:
                        dve.wait_ge(yev, reads)
                        v.tensor_tensor(acc[par][:], acc[par][:], z[:], ALU.add).then_inc(zfin if e == E - 1 else yadd, 1)

                def update(i, tp, par, fin=False):
                    dve.wait_ge(yT_ps, i + 1)
                    for b in range(NB):
                        ub = u[:, ds(tp * TILE + b * P, P)]
                        last = v.scalar_tensor_tensor(fu[par][:, b * P:(b + 1) * P] if fin else ub, ub, csum[par][:, b:b + 1], ps_t[:, b * P:(b + 1) * P], ALU.mult, ALU.add)
                    last.then_inc(upd, 1)

                def prep_stats(t, n):
                    for b in range(NB):
                        last = v.bn_stats(bn[:, b, :], u[:, ds(t * TILE + b * P, P)])
                    last.then_inc(p_bn, 1)

                def prep_aggr(n):
                    dve.wait_ge(p_bn, n + 1).then_inc(s_alone, 1)
                    for b in range(NB):
                        last = v.bn_aggr(mv[:, b, :], bn[:, b, :])
                    last.then_inc(p_mv, 1)

                def prep_norm(t, n):
                    dve.wait_ge(p_rs, n + 1)
                    for b in range(NB):
                        last = v.tensor_scalar(xh[:, b * P:(b + 1) * P], u[:, ds(t * TILE + b * P, P)], mv[:, b, 0:1],
                                               rs[:, b:b + 1], ALU.subtract, ALU.mult)
                    last.then_inc(p_xh, 1)

                def prep_rest(n, par):
                    dve.wait_ge(p_xhi, n + 1)
                    v.tensor_tensor(xTl[par][:], ps_t[:], xTh[par][:].bitcast(F32), ALU.subtract).then_inc(p_xlo, 1)

                def over_blocks(ap):
                    return ap.unsqueeze(1).to_broadcast([P, NB, E])

                def over_experts(ap):
                    return ap.unsqueeze(2).to_broadcast([P, NB, E])

                def link(n, k):
                    dve.wait_ge(p_link, n * LINKS + k)

                def router_logits(l, n):
                    dve.wait_ge(p_lg_ps, n + 1)
                    dve.wait_ge(p_sd, n + 1)
                    v.reduce_sum(lg[:], ps_r[:, LG].rearrange("p (b h e) -> p b e h", b=NB, h=2), axis=AX.X).then_inc(p_link, 1)
                    v.tensor_tensor(t2[:], mv[:, :, 0:1].to_broadcast([P, NB, E]), over_blocks(cs[:, ds(l * E, E)]), ALU.mult)
                    link(n, 1)
                    v.tensor_tensor(t1[:], lg[:], over_experts(sd[:]), ALU.mult).then_inc(p_link, 1)
                    link(n, 2)
                    v.tensor_tensor(t3[:], t1[:], t2[:], ALU.add).then_inc(p_link, 1)
                    link(n, 3)
                    v.tensor_tensor(lgf[:], t3[:], over_blocks(rb[:, ds(l * E, E)]), ALU.add).then_inc(p_link, 1)

                def router_rank(n):
                    link(n, 4)
                    v.tensor_tensor(dd[:], lgf[:].unsqueeze(2).to_broadcast([P, NB, E, E]),
                                    lgf[:].unsqueeze(3).to_broadcast([P, NB, E, E]), ALU.subtract).then_inc(p_link, 1)
                    link(n, 5)
                    v.tensor_tensor(cc[:].rearrange("p b e f -> p b (e f)"), dd[:].rearrange("p b e f -> p b (e f)"),
                                    order[:].unsqueeze(1).to_broadcast([P, NB, E * E]), ALU.is_ge).then_inc(p_link, 1)
                    link(n, 6)
                    v.reduce_sum(rank[:], cc[:], axis=AX.X).then_inc(p_link, 1)
                    link(n, 7)
                    v.tensor_scalar(first[:], rank[:], 0.0, None, ALU.is_equal)
                    v.tensor_scalar(top2[:], rank[:], 2.0, 0.5, ALU.is_lt, ALU.mult).then_inc(p_link, 1)

                def router_difference(n):
                    link(n, 8)
                    v.scalar_tensor_tensor(second_first[:], rank[:], 1.0, first[:], ALU.is_equal, ALU.subtract).then_inc(p_link, 1)
                    link(n, 9)
                    v.tensor_tensor(signed[:], second_first[:], lgf[:], ALU.mult).then_inc(p_link, 1)
                    link(n, 10)
                    v.reduce_sum(ndiff[:], signed[:], axis=AX.X).then_inc(p_nd, 1)

                def router_shares(n, par):
                    dve.wait_ge(p_th, n + 1)
                    v.scalar_tensor_tensor(shift[:], second_first[:], -0.5, over_experts(th[:]), ALU.mult, ALU.mult).then_inc(p_link, 1)
                    link(n, 11)
                    v.tensor_tensor(comb[:].rearrange("p e b -> p b e"), shift[:], top2[:], ALU.add).then_inc(p_comb, 1)
                    dve.wait_ge(p_comb, n + 1)
                    v.reduce_sum(csum[par][:], comb[:].rearrange("p e b -> p b e"), axis=AX.X).then_inc(p_sum, 1)

                def rest_w1(l, e, n):
                    dve.wait_ge(c1h, n)
                    v.scalar_tensor_tensor(w1l[:, e * F:(e + 1) * F], w1s[:, e * F:(e + 1) * F], cols[:, ds(l * E + e + LNG, 1)],
                                           w1h[:, e * F:(e + 1) * F].bitcast(F32), ALU.mult, ALU.subtract).then_inc(c1, 1)

                def rest_w2(e, n):
                    dve.wait_ge(c2h, n)
                    v.tensor_tensor(w2l[:, e * F:(e + 1) * F], w2s[:, e * F:(e + 1) * F],
                                    w2h[:, e * F:(e + 1) * F].bitcast(F32), ALU.subtract).then_inc(c2, 1)

                def finish_stats(t, i, par):
                    dve.wait_ge(upd, i + 2).then_inc(s_alone, 1)
                    for b in range(NB):
                        last = v.bn_stats(fbn[:, b, :], fu[par][:, b * P:(b + 1) * P])
                    last.then_inc(f_bn, 1)
                    if not isinstance(t, int) or t > 0:
                        dve.wait_ge(f_n, t).then_inc(s_alone, 1)
                    dve.wait_ge(f_bn, t + 1).then_inc(s_alone, 1)
                    for b in range(NB):
                        last = v.bn_aggr(fmv[:, b, :], fbn[:, b, :])
                    last.then_inc(f_mv, 1)

                def combine_before(i, e, par):
                    bcol = (i + NT - 1) // NT * E + B2 - E
                    combine(None, e, par, bcol, i * (K // 2) - 6 + 2 * e + PAIRS, i * E + e - 1, i * 2 + e - 1)

                def step(l, t, par, start=False, end=False, fin=False, nxt=True):
                    i = l * NT + t
                    tp = (i + NT - 1) % NT
                    tn, ln = (0, l + 1) if end else (t + 1, l)
                    for j in range(K // 2):
                        rest(i, j)
                        if j == 0 and nxt:
                            prep_stats(tn, i + 1)
                        if j == 1:
                            if nxt:
                                prep_aggr(i + 1)
                            combine_before(i, 2, 1 - par)
                        if j == 2 and nxt:
                            prep_norm(tn, i + 1)
                        if j == 3:
                            combine_before(i, 3, 1 - par)
                        if j == 4 and nxt:
                            prep_rest(i + 1, 1 - par)
                        if j == 5:
                            combine(i, 0, par, l * E + B2, i * (K // 2) + 2 + PAIRS, None, None)
                            if nxt:
                                router_logits(ln, i + 1)
                        if j == 6:
                            if nxt:
                                router_rank(i + 1)
                                router_difference(i + 1)
                            update(i, tp, 1 - par, fin)
                            if fin:
                                finish_stats(t - 1, i, 1 - par)
                        if j == 7:
                            combine(i, 1, par, l * E + B2, i * (K // 2) + 4 + PAIRS, i * E + 4, i + 1)
                            if nxt:
                                router_shares(i + 1, 1 - par)
                        if end and j % 2 == 1:
                            rest_w1(l + 1, j // 2, l * E + E + j // 2 + 1)
                        if end and j in (5, 7):
                            rest_w2((j - 5) // 2, l * E + E + (j - 5) // 2 + 1)
                        if start and j in (4, 6):
                            e = 2 if j == 4 else 3
                            rest_w2(e, l * E + e + 1)

                dve.sem_inc(lo, PAIRS)
                dve.sem_inc(yadd, 1)
                dve.sem_inc(upd, 1)
                prep_stats(0, 0)
                prep_aggr(0)
                v.memset(ps_y[0][:], 0.0)
                v.memset(ps_y[1][:], 0.0).then_inc(s_zero, 1)
                rwv = rw[:].rearrange("p (l e) -> p l e", l=L)
                rpv = rwp[:].rearrange("p (l h e) -> p l h e", l=L, h=2)
                v.tensor_copy(rpv[:, :, 0, :], rwv).then_inc(s_whi, 1)
                dve.wait_ge(s_whi, 1)
                v.tensor_tensor(rpv[:, :, 1, :], rwv, rpv[:, :, 0, :].bitcast(F32), ALU.subtract).then_inc(s_rwp, 1)
                rest_w1(0, 0, 1)
                prep_norm(0, 0)
                rest_w1(0, 1, 2)
                prep_rest(0, 0)
                rest_w1(0, 2, 3)
                rest_w1(0, 3, 4)
                router_logits(0, 0)
                router_rank(0)
                router_difference(0)
                rest_w2(0, 1)
                rest_w2(1, 2)
                router_shares(0, 0)
                dve.wait_ge(s_zero, 2)
                steps(dve, step)
                i = L * NT
                combine_before(i, 2, 1)
                combine_before(i, 3, 1)
                update(i, NT - 1, 1, True)
                finish_stats(NT - 1, i, 1)

            @block.tensor
            def _(pe):
                mm = nc.tensor.matmul

                def blk(b):
                    return slice(b * P, (b + 1) * P)

                def first(i, k, par):
                    n = k % BANKS
                    if k == 0:
                        pe.wait_ge(p_xlo, i + 1)
                    pe.wait_ge(gel, i * K + k + 1)
                    c = slice(k * P, (k + 1) * P)
                    mm(ps_h[n][:], w1h[:, c], xTh[par][:], start=True, stop=False)
                    mm(ps_h[n][:], w1h[:, c], xTl[par][:], start=False, stop=False)
                    mm(ps_h[n][:], w1l[:, c], xTh[par][:], start=False, stop=True).then_inc(s1, 1)

                def second(i, k):
                    e = k // FC
                    if k % FC == 0:
                        pe.wait_ge(yev, i * E + e + 1)
                    if k % 2 == 0:
                        pe.wait_ge(lo, i * (K // 2) + k // 2 + 1 + PAIRS)
                    c = slice(k * P, (k + 1) * P)
                    h = slice(k % 2 * TILE, (k % 2 + 1) * TILE)
                    y, n = ps_y[e % 2], k // 2 % PAIRS
                    mm(y[:], w2h[:, c], hh[n][:, h], start=k % FC == 0, stop=False)
                    mm(y[:], w2h[:, c], hl[n][:, h], start=False, stop=False)
                    last = mm(y[:], w2l[:, c], hh[n][:, h], start=False, stop=k % FC == FC - 1)
                    if k % 2:
                        last.then_inc(s2, 1)

                def y_tokens(i, par):
                    pe.wait_ge(zfin, i + 1)
                    for b in range(NB):
                        last = nc.tensor.transpose(ps_t[:, blk(b)], acc[par][:, blk(b)], ident[:])
                    last.then_inc(yT_ps, 1)

                def prep_x(n):
                    pe.wait_ge(p_xh, n + 1)
                    for b in range(NB):
                        last = nc.tensor.transpose(ps_t[:, blk(b)], xh[:, blk(b)], ident[:])
                    last.then_inc(p_xT_ps, 1)

                def prep_logits(l, n, par):
                    pe.wait_ge(p_xlo, n + 1)
                    if not isinstance(n, int) or n > 0:
                        pe.wait_ge(p_cT, n)
                    w = rwp[:, ds(l * 2 * E, 2 * E)]
                    for b in range(NB):
                        o = ps_r[:, b * 2 * E:(b + 1) * 2 * E]
                        mm(o, xTh[par][:, blk(b)], w, start=True, stop=False)
                        last = mm(o, xTl[par][:, blk(b)], w, start=False, stop=True)
                    last.then_inc(p_lg_ps, 1)

                def prep_combT(n):
                    pe.wait_ge(p_comb, n + 1)
                    nc.tensor.transpose(ps_r[0:E * NB, CT], comb[:].rearrange("p e b -> p (e b)"), ident[:]).then_inc(p_cT_ps, 1)

                def step(l, t, par, start=False, end=False, fin=False, nxt=True):
                    i = l * NT + t
                    ln = l + 1 if end else l
                    for k in range(K):
                        if k == 0:
                            pe.wait_ge(c1, l * E + E)
                            pe.wait_ge(c2, l * E + 2)
                        if start and k in (2 * FC, 3 * FC):
                            pe.wait_ge(c2, l * E + k // FC + 1)
                        if k < K - LEAD:
                            first(i, k + LEAD, par)
                        elif nxt:
                            k1 = k + LEAD - K
                            if end and k1 % FC == 0:
                                pe.wait_ge(c1, l * E + E + k1 // FC + 1)
                            first(i + 1, k1, 1 - par)
                        second(i, k)
                        if k == 1 and nxt:
                            pe.wait_ge(upd, i + 1)
                            prep_x(i + 1)
                        if k == 4 and nxt:
                            prep_logits(ln, i + 1, 1 - par)
                        if k == 6:
                            y_tokens(i, 1 - par)
                        if k == 12 and nxt:
                            prep_combT(i + 1)

                pe.sem_inc(s2, PAIRS)
                prep_x(0)
                pe.wait_ge(s_rwp, 1)
                for k in range(LEAD):
                    if k % FC == 0:
                        pe.wait_ge(c1, k // FC + 1)
                    first(0, k, 0)
                    if k == BANKS - 1:
                        prep_logits(0, 0, 0)
                prep_combT(0)
                steps(pe, step)
                y_tokens(L * NT, 1)


_INS = ['L0_attn_x', 'L0_attn_wqkv', 'L0_attn_wo', 'L0_ffn_router_w', 'L0_ffn_router_b', 'L0_ffn_ln_g', 'L0_ffn_ln_b',
        'L0_ffn_w1', 'L0_ffn_b1', 'L0_ffn_w2', 'L0_ffn_b2']
_OUT = (BATCH, SEQ, D)


def kernel(**inputs):
    import numpy as _np
    import concourse.bacc as _bacc
    from concourse import mybir as _mybir
    from concourse.bass_utils import run_bass_kernel_spmd as _run

    nc = _bacc.Bacc("TRN2", target_bir_lowering=False, num_devices=1)
    arrays, args = {}, []
    for name in _INS:
        a = _np.ascontiguousarray(inputs[name])
        arrays[f"in_{name}_dram"] = a
        args.append(nc.dram_tensor(f"in_{name}_dram", a.shape, _mybir.dt.from_np(a.dtype), kind="ExternalInput").ap())
    args.append(nc.dram_tensor("out_0_dram", _OUT, F32, kind="ExternalOutput").ap())
    sandwich_kernel(nc, *args)
    r = _run(nc, [arrays], core_ids=[0])
    return r.results[0]["out_0_dram"]
```
